# Optimizing a Trainium2 kernel written in Bass

```python
import numpy as np
import jax
import jax.numpy as jnp

def _softmax(x, axis=-1):
    return jax.nn.softmax(x, axis=axis)

def _gelu(x):
    return jax.nn.gelu(x, approximate=True)

def _silu(x):
    return jax.nn.silu(x)

def _sigmoid(x):
    return jax.nn.sigmoid(x)

def _layernorm(x, axis=-1, eps=1e-05):
    m = jnp.mean(x, axis=axis, keepdims=True)
    v = jnp.var(x, axis=axis, keepdims=True)
    return (x - m) / jnp.sqrt(v + eps)

def _scatter_add(tgt, idx, src, axis=0):
    return tgt.at[idx].add(src)

def _segment_sum(src, seg, n):
    return jax.ops.segment_sum(src, seg, n)
kernel_name = 'mk_gnn_resnorm_d1_gnn_r64_c692fb'

def setup_inputs(seed: int=0):
    np.random.seed(seed)
    _w = jnp.asarray

    def _rec_inputs():
        import jax
        import jax.numpy as jnp
        _gk = jax.random.key(seed)
        x = -0.000202 + 1 * jax.random.normal(jax.random.fold_in(_gk, 1), (50000, 64), jnp.float32)
        src = jax.random.randint(jax.random.fold_in(_gk, 2), (25000,), 0, 50000, jnp.int32)
        dst = jnp.minimum((50000 * jax.random.uniform(jax.random.fold_in(_gk, 3), (25000,)) ** 2.0).astype(jnp.int32), 49999)
        _o = jnp.argsort(dst, stable=True)
        src = src[_o]
        dst = dst[_o]
        edge_attr_64 = -6.74381e-05 + 0.999835 * jax.random.normal(jax.random.fold_in(_gk, 12), (25000, 64), jnp.float32)
        edge_type_10 = jax.random.randint(jax.random.fold_in(_gk, 13), (25000,), 0, 10, jnp.int32)
        return (x, src, dst, edge_attr_64, edge_type_10)
    x, src, dst, edge_attr_64, edge_type_10 = _rec_inputs()

    def _L0_gnn_setup():
        import jax, jax.numpy as jnp
        import numpy as np
        NEG_SLOPE = 0.01
        N_NODES = 100000
        N_EDGES = 1250000
        N_REL = 10
        D = 64
        key = jax.random.key(seed)
        ks = jax.random.split(key, 8)
        return {'nfeat': jax.random.normal(ks[0], (N_NODES, D), dtype=jnp.float32), 'efeat': jax.random.normal(ks[1], (N_EDGES, D), dtype=jnp.float32), 'relation_weight': jax.random.normal(ks[2], (N_REL, D, D), dtype=jnp.float32) * (1.0 / np.sqrt(D)), 'res_fc_w': jax.random.normal(ks[3], (D, D), dtype=jnp.float32) * (1.0 / np.sqrt(D)), 'res_fc2_w': jax.random.normal(ks[4], (D, D), dtype=jnp.float32) * (1.0 / np.sqrt(D)), 'src': jax.random.randint(ks[5], (N_EDGES,), 0, N_NODES, dtype=jnp.int32), 'dst': jnp.sort(jax.random.randint(ks[6], (N_EDGES,), 0, N_NODES, dtype=jnp.int32)), 'etype': jax.random.randint(ks[7], (N_EDGES,), 0, N_REL, dtype=jnp.int32)}
    _L0_gnn_all = _L0_gnn_setup()
    _L0_gnn_in = {k: v for k, v in _L0_gnn_all.items() if k in ('relation_weight', 'res_fc_w', 'res_fc2_w')}
    del _L0_gnn_all
    return {'x': x, 'src': src, 'dst': dst, 'edge_attr_64': edge_attr_64, 'edge_type_10': edge_type_10, 'L0_gnn_relation_weight': _L0_gnn_in['relation_weight'], 'L0_gnn_res_fc_w': _L0_gnn_in['res_fc_w'], 'L0_gnn_res_fc2_w': _L0_gnn_in['res_fc2_w']}

def reference(x, src, dst, edge_attr_64, edge_type_10, L0_gnn_relation_weight, L0_gnn_res_fc_w, L0_gnn_res_fc2_w):
    import jax
    import jax.numpy as jnp

    def _L0_gnn_ref(nfeat, efeat, relation_weight, res_fc_w, res_fc2_w, src, dst, etype):
        import jax, jax.numpy as jnp
        import numpy as np
        NEG_SLOPE = 0.01
        N_NODES = 100000
        N_EDGES = 1250000
        N_REL = 10
        D = 64
        n = nfeat.shape[0]
        proj = jnp.einsum('ni,rio->nro', nfeat, relation_weight)
        t_r = proj[src, etype]
        h_r = proj[dst, etype]
        att = jnp.sum(t_r * jnp.tanh(h_r + efeat), axis=-1)
        seg_max = jax.ops.segment_max(att, dst, num_segments=n)
        ex = jnp.exp(att - seg_max[dst])
        seg_sum = jax.ops.segment_sum(ex, dst, num_segments=n)
        a = ex / seg_sum[dst]
        h_nb = jax.ops.segment_sum(nfeat[src] * a[:, None], dst, num_segments=n)
        out = jax.nn.leaky_relu((nfeat + h_nb) @ res_fc_w.T, NEG_SLOPE) + jax.nn.leaky_relu(nfeat * h_nb @ res_fc2_w.T, NEG_SLOPE)
        return out
    x = _layernorm(x + _L0_gnn_ref(x, edge_attr_64, L0_gnn_relation_weight, L0_gnn_res_fc_w, L0_gnn_res_fc2_w, src, dst, edge_type_10), axis=-1)
    return x

_drawn_inputs = setup_inputs


def setup_inputs(seed=0):
    import zlib

    import numpy as np

    out = dict(_drawn_inputs(seed))
    spreads = {}
    factors = {}
    for name, (base, spread) in spreads.items():
        noise = np.random.default_rng([zlib.crc32(name.encode()), seed]).standard_normal(out[name].shape)
        drawn = base * np.exp(spread * noise) if base else spread * noise
        out[name] = jnp.asarray(drawn.astype(out[name].dtype))
    for name, factor in factors.items():
        out[name] = (out[name] * factor).astype(out[name].dtype)
    return out
```

```python
from contextlib import ExitStack

import concourse.bass as bass
from concourse import mybir

ALU = mybir.AluOpType
ACT = mybir.ActivationFunctionType
AX = mybir.AxisListType
F32 = mybir.dt.float32
BF16 = mybir.dt.bfloat16
I32 = mybir.dt.int32

P = 128
DMA = 16
TG = 4
RING = 4
BIG = 3.0e38
NONE = 1.0e30
FAR = 1 << 20
SLOPE = 0.01
EPS = 1e-5
MAGIC = 0x5F3759DF
XM = 4


class Group:

    def __init__(self, turn, slot):
        self.turn, self.slot = turn, slot
        self.n = turn * RING + slot

    def back(self, k):
        turn, slot = self.turn, self.slot - k
        while slot < 0:
            turn, slot = turn - 1, slot + RING
        return Group(turn, slot)


def known(v):
    return isinstance(v, int)


def wait(eng, sem, value):
    if not known(value) or value > 0:
        eng.wait_ge(sem, value)


def hold(pool, tile, done, g):
    wait(pool, done, g.n - RING + 1)
    pool.tensor_tensor(tile[:, g.slot + 1:g.slot + 2], tile[:, 0:1], tile[:, 0:1], ALU.add).then_inc(done, 1)


def run_groups(eng, step, groups, lag, first=None):
    if first is None:
        first = 1 if lag == 0 else 2
    last = groups // RING
    for it in range(first * RING):
        step(Group(it // RING, it % RING))
    with eng.Fori(first, last) as turn:
        for slot in range(RING):
            step(Group(turn, slot))
    for it in range(last * RING, groups + lag):
        step(Group(it // RING, it % RING))


def gnn_resnorm(nc, x, src, dst, eattr, etype, relw, resw, resw2, out):
    N, D = x.shape
    E = src.shape[0]
    R = relw.shape[0]
    T = -(-E // P)
    NG = T // TG
    assert T % TG == 0 and D == 64 and R % 2 == 0
    NK = R // 2
    LASTC = E - (P - 1) * T
    W = TG * P
    DR = -(-N // (NG * P))
    DB = P * DR
    DLAST = N - (NG - 1) * DB
    assert DR % 2 == 0 and DR * D == 512 and DLAST % DR == 0 and 0 < LASTC < T
    PL = DLAST // DR
    PL0 = PL // DMA * DMA

    with ExitStack() as ctx:
        def sb(name, shape, dt=F32):
            return ctx.enter_context(nc.sbuf_tensor(name, shape, dt))

        def ps(name, shape):
            return ctx.enter_context(nc.psum_tensor(name, shape, F32))

        def sem(name):
            return ctx.enter_context(nc.semaphore(name))

        ident = sb("ident", [P, P])
        identb = sb("identb", [P, P], BF16)
        ones = sb("ones", [P, 1])
        relk0 = sb("relk0", [P, NK])
        relk = sb("relk", [P, NK])
        before = sb("before", [P, P])
        w_pair = sb("w_pair", [P, NK, D])
        res_rows = sb("res_rows", [D, 3 * D])
        bd_res = sb("bd_res", [P, P])
        bd_mix = sb("bd_mix", [P, P])
        bd_both = sb("bd_both", [P, P])
        st_mix = sb("st_mix", [P, D])
        ends_i = sb("ends_i", [P, 2, T], I32)
        next_i = sb("next_i", [P, 2], I32)
        type_i = sb("type_i", [P, T], I32)
        type_b = sb("type_b", [P, T], BF16)
        dst_f0 = sb("dst_f0", [P, T + 1])
        dst_f = sb("dst_f", [P, T + 1])
        same = sb("same", [P, T])
        start = sb("start", [P, T])
        row_i = sb("row_i", [P, T], I32)
        inf_f = sb("inf_f", [P, T])
        m_all = sb("m_all", [P, T + 1])
        s_all = sb("s_all", [P, T + 1])
        es_all = sb("es_all", [P, T + 1, D])
        xd_all = sb("xd_all", [P, T, D])
        idx = sb("idx", [P, RING, 2, TG], I32)
        x_r = sb("x_r", [P, RING, 2, TG, 2, D])
        e_r = sb("e_r", [P, RING, TG, D])
        xT = sb("xT", [P, 2, 2, W])
        typ = sb("typ", [P, 2, W])
        xm = sb("xm", [P, XM, 2, W])
        g_r = sb("g_r", [D, 2, W])
        prod = sb("prod", [D, 2, W])
        delta = sb("delta", [P, 2, 2, TG])
        wd = sb("wd", [P, 2, 2, TG])
        wx = sb("wx", [P, 2, TG, D])
        x_in = sb("x_in", [P, RING, DR * D])
        dT = sb("dT", [P, 2, 512])
        relu = sb("relu", [P, 2, 512])
        z = sb("z", [P, RING, DR * D])
        o = sb("o", [P, 2, DR * D])
        junk = sb("junk", [P, 2, DR * D])
        held = sb("held", [P, 2, RING + 1])
        newt = sb("newt", [P, 2, DR])
        row_r = sb("row_r", [P, RING, TG], I32)
        out_r = sb("out_r", [P, RING, TG, D])
        prev = sb("prev", [P, 8])
        carry = sb("carry", [P, D + 1])
        zsum = sb("zsum", [P, RING, DR])
        nmean = sb("nmean", [P, RING, DR])
        ssq = sb("ssq", [P, RING, DR])
        var = sb("var", [P, RING, DR])
        rstd = sb("rstd", [P, RING, DR])
        nbias = sb("nbias", [P, RING, DR])

        xT_ps = ps("xT_ps", [P, 2, W])
        typ_ps = ps("typ_ps", [P, W])
        th_ps = ps("th_ps", [P, W])
        att_ps = ps("att_ps", [P, 512])
        dT_ps = ps("dT_ps", [P, 512])
        y_ps = ps("y_ps", [P, 2, 512])

        tab = x_in.rearrange("p a b -> p (a b)")
        mats = e_r.rearrange("p a b f -> p (a b f)")[:, 0:5 * P].rearrange("p (k q) -> p k q", q=P)
        prod_ex = o.rearrange("p a (k f) -> p a k f", k=2)
        fa, fb = tab[:, 0:T], tab[:, T:2 * T]

        tables_zero, tables_in, w_in, e_in = sem("tables_zero"), sem("tables_in"), sem("w_in"), [sem("e_in0"), sem("e_in1")]
        twice, sub_done, e_zero = sem("twice"), sem("sub_done"), sem("e_zero")
        consts, dst_masked = sem("consts"), sem("dst_masked")
        setup_v, resT = sem("setup_v"), sem("resT")
        idx_in = [sem(f"idx_in{i}") for i in range(RING)]
        e_staged = [sem(f"e_staged{i}") for i in range(RING)]
        gathered = [sem(f"gathered{i}") for i in range(RING)]
        xd_saved = [sem(f"xd_saved{i}") for i in range(RING)]
        x_loaded = [sem(f"x_loaded{i}") for i in range(RING)]
        o_stored = [sem(f"o_stored{i}") for i in range(2)]
        xT_done, xT_out, typ_done, typ_out = sem("xT_done"), sem("xT_out"), sem("typ_done"), sem("typ_out")
        masked, pair_done, main_done = sem("masked"), sem("pair_done"), sem("main_done")
        tanh_done, prod_done, att_done, max_done = sem("tanh_done"), sem("prod_done"), sem("att_done"), sem("max_done")
        delta_done, exp_done, wx_done, sum_step, den_done = (
            sem("delta_done"), sem("exp_done"), sem("wx_done"), sem("sum_step"), sem("den_done"))
        dT_done, dT_out, y_done, relu_done, z_done = (
            sem("dT_done"), sem("dT_out"), sem("y_done"), sem("relu_done"), sem("z_done"))
        held_gather, held_scatter = sem("held_gather"), sem("held_scatter")
        newt_step, dense_stored = sem("newt_step"), sem("dense_stored")
        ex_pe, ex_v, ex_w, ex_act = sem("ex_pe"), sem("ex_v"), sem("ex_w"), sem("ex_act")
        scattered = [sem(f"scattered{i}") for i in range(RING)]
        row_done, h_step, uw_done, uwT_done, uwT_out, y3_done, relu3_done, za_done, z3_done, zsum3_done = (
            sem(n) for n in ["row_done", "h_step", "uw_done", "uwT_done", "uwT_out", "y3_done", "relu3_done", "za_done",
                             "z3_done", "zsum3_done"])
        mean3_done, sq3_done, var3_done, sqrt3_done, rec3_done, bias3_done, norm3_done = (
            sem(n) for n in ["mean3_done", "sq3_done", "var3_done", "sqrt3_done", "rec3_done", "bias3_done", "norm3_done"])
        zsum_done, mean_done, ssq_done, var_done, rstd_done, bias_done, norm_done = (
            sem("zsum_done"), sem("mean_done"), sem("ssq_done"), sem("var_done"), sem("rstd_done"),
            sem("bias_done"), sem("norm_done"))

        SETUP_V = 22
        E0 = 8 * TG

        def live(g, k=0):
            return not known(g.turn) or 0 <= g.n - k < NG

        def x_block(d, part=slice(0, P)):
            return x[bass.ds(d.n * DB, DB), :].rearrange("(p j) f -> p (j f)", j=DR)

        def dense_dma(eng, to_sbuf, d, tile, done):
            dram = x if to_sbuf else out
            if known(d.turn) and d.n == NG - 1:
                parts = [(0, PL0), (PL0, PL)] if PL0 < PL else [(0, PL)]
            else:
                parts = [(0, P)]
            for a, b in parts:
                rows = dram[bass.ds(d.n * DB + a * DR, (b - a) * DR), :].rearrange("(p j) f -> p (j f)", j=DR)
                if to_sbuf:
                    eng.dma_start(tile[a:b, :], rows).then_inc(done, DMA)
                else:
                    eng.dma_start(rows, tile[a:b, :]).then_inc(done, DMA)

        def dense_dmas(d):
            return DMA if known(d.turn) and d.n == NG - 1 and PL0 < PL else 0

        ctx2 = ctx.enter_context(nc.Block())
        block = ctx2

        @block.sync
        def _(sp):
            def table(dram, tile):
                rows = dram[0:(P - 1) * T].rearrange("(p c) -> p c", c=T)
                a = (P - 1) // DMA * DMA
                sp.dma_start(tile[0:a, 0:T], rows[0:a, :]).then_inc(tables_in, DMA)
                sp.dma_start(tile[a:P - 1, 0:T], rows[a:P - 1, :]).then_inc(tables_in, DMA)
                sp.dma_start(tile[P - 1:P, 0:LASTC], dram[(P - 1) * T:E].rearrange("(a c) -> a c", a=1)).then_inc(tables_in, DMA)
            sp.wait_ge(tables_zero, 3)
            table(src, ends_i[:, 0, :])
            table(dst, ends_i[:, 1, :])
            table(etype, type_i[:, :])
            heads = dst[T:(P - 1) * T].rearrange("(p c) -> p c", c=T)
            sp.dma_start(next_i[0:P - 2, :], heads[:, 0:2]).then_inc(tables_in, DMA)
            sp.dma_start(next_i[P - 2:P - 1, :], dst[(P - 1) * T:(P - 1) * T + 2].rearrange("(a c) -> a c", a=1)).then_inc(tables_in, DMA)
            for h in range(2):
                sp.dma_start(w_pair[h * D:(h + 1) * D, :, :],
                             relw.rearrange("(k h) i o -> h i k o", h=2)[h]).then_inc(w_in, DMA)
            for n, w in enumerate([resw, resw, resw2]):
                sp.dma_start(res_rows[:, n * D:(n + 1) * D], w[:, :]).then_inc(w_in, DMA)
            rows = eattr[0:(P - 1) * T, :].rearrange("(p c) f -> p c f", c=T)
            a = (P - 1) // DMA * DMA
            last = eattr[(P - 1) * T:E, :].rearrange("(a c) f -> a c f", a=1)
            sp.wait_ge(e_zero, 1)
            for n, (c0, c1) in enumerate([(0, E0), (E0, T)]):
                c2 = min(c1, LASTC)
                sp.dma_start(es_all[0:a, c0 + 1:c1 + 1, :], rows[0:a, c0:c1, :]).then_inc(e_in[n], DMA)
                sp.dma_start(es_all[a:P - 1, c0 + 1:c1 + 1, :], rows[a:P - 1, c0:c1, :]).then_inc(e_in[n], DMA)
                sp.dma_start(es_all[P - 1:P, c0 + 1:c2 + 1, :], last[:, c0:c2, :]).then_inc(e_in[n], DMA)
            sp.wait_ge(tables_in, 11 * DMA)

            def step(g):
                if live(g):
                    wait(sp, gathered[g.slot], g.turn * 2 * TG * DMA)
                    sp.dma_start(idx[:, g.slot, :, :], ends_i[:, :, bass.ds(g.n * TG, TG)]).then_inc(idx_in[g.slot], DMA)
                    wait(sp, z_done, g.n - RING + 1)
                    dense_dma(sp, True, g, x_in[:, g.slot, :], x_loaded[g.slot])
                    if known(g.turn) and g.n in (0, 7):
                        sp.wait_ge(e_in[min(g.n, 1)], 3 * DMA)
                    wait(sp, main_done, g.n - RING + 1)
                    sp.dma_start(e_r[:, g.slot, :, :], es_all[:, bass.ds(g.n * TG + 1, TG), :]).then_inc(e_staged[g.slot], DMA)
            run_groups(sp, step, NG, 0, first=2)

        @block.gpsimd
        def _(pool):
            pool.memset(ones[:, :], 1.0).then_inc(consts, 1)
            pool.memset(held[:, :, 0:1], 0.0).then_inc(consts, 1)
            pool.memset(ident[:, :], 0.0).then_inc(consts, 1)
            pool.memset(before[:, :], 1.0).then_inc(consts, 1)
            pool.iota(relk0[:, :], [[2, NK]], base=0, channel_multiplier=0,
                      allow_small_or_imprecise_dtypes=True).then_inc(consts, 1)
            pool.wait_ge(consts, 5)
            pool.affine_select(ident[:, :], ident[:, :], [[-1, P]], ALU.not_equal, 1.0, base=0,
                               channel_multiplier=1).then_inc(consts, 1)
            pool.affine_select(before[:, :], before[:, :], [[-1, P]], ALU.is_ge, 0.0, base=-1,
                               channel_multiplier=1).then_inc(consts, 1)

            def step(g):
                if live(g):
                    pool.wait_ge(idx_in[g.slot], (g.turn + 1) * DMA)
                    wait(pool, wx_done, g.n - RING + 1)
                    wait(pool, xd_saved[g.slot], g.turn * DMA)
                    hold(pool, held[:, 0, :], held_gather, g)
                if live(g):
                    for j in range(TG):
                        for side in range(2):
                            pool.indirect_dma_start(
                                x_r[:, g.slot, side, j, 0, :], None, x[:, :],
                                bass.IndirectOffsetOnAxis(ap=idx[:, g.slot, side, j:j + 1], axis=0),
                            ).then_inc(gathered[g.slot], DMA)
                if known(g.turn) and g.n == 0:
                    pool.wait_ge(setup_v, 2)
                    pool.affine_select(dst_f[:, :], dst_f0[:, :], [[-1, T + 1]], ALU.is_ge, float(FAR),
                                       base=E - 1, channel_multiplier=-T).then_inc(dst_masked, 1)
            run_groups(pool, step, NG, 0)

            def scatter(g):
                pool.wait_ge(row_done, g.n + 1)
                pool.wait_ge(norm3_done, g.n + 1)
                hold(pool, held[:, 1, :], held_scatter, g)
                for j in range(TG):
                    pool.indirect_dma_start(
                        out[:, :], bass.IndirectOffsetOnAxis(ap=row_r[:, g.slot, j:j + 1], axis=0),
                        out_r[:, g.slot, j, :], None, bounds_check=top, oob_is_err=False,
                    ).then_inc(scattered[g.slot], DMA)
            pool.wait_ge(dense_stored, 1)
            top = pool.to_reg(N - 1)
            run_groups(pool, scatter, NG, 0)
            for q in range(RING):
                pool.wait_ge(scattered[q], -(-(NG - q) // RING) * TG * DMA)

        @block.tensor
        def _(pe):
            pe.wait_ge(w_in, 5 * DMA)
            pe.wait_ge(consts, 7)
            pe.transpose(att_ps[:, 0:D], res_rows[:, 0:2 * D], ident[0:D, 0:D])
            pe.transpose(att_ps[:, D:2 * D], res_rows[:, D:3 * D], ident[0:D, 0:D]).then_inc(resT, 1)
            pe.wait_ge(setup_v, SETUP_V)

            def turn_in(g):
                pe.wait_ge(twice, g.n + 1)
                wait(pe, xT_out, 2 * g.n)
                for side in range(2):
                    for j in range(TG):
                        mm = pe.transpose(xT_ps[:, side, j * P:(j + 1) * P],
                                          x_r[:, g.slot, side, j, :, :].rearrange("p a f -> p (a f)"), ident[:, :])
                    mm.then_inc(xT_done, 1)
                wait(pe, typ_out, g.n)
                for j in range(TG):
                    mm = pe.matmul(typ_ps[:, j * P:(j + 1) * P],
                                   type_b[:, bass.ds(g.n * TG + j, 1)].to_broadcast([P, P]), identb[:, :],
                                   start=True, stop=True)
                mm.then_inc(typ_done, 1)

            def dense_turn(d):
                pe.wait_ge(x_loaded[d.slot], (d.turn + 1) * DMA + dense_dmas(d))
                wait(pe, dT_out, d.n)
                for j in range(DR // 2):
                    mm = pe.transpose(dT_ps[:, j * P:(j + 1) * P], x_in[:, d.slot, j * P:(j + 1) * P], ident[:, :])
                mm.then_inc(dT_done, 1)

            def dense_y(d):
                pe.wait_ge(dT_out, d.n + 1)
                wait(pe, z_done, d.n)
                for j in range(DR // 2):
                    for n, w in enumerate([bd_res, bd_mix]):
                        mm = pe.matmul(y_ps[:, n, j * P:(j + 1) * P], dT[:, d.slot % 2, j * P:(j + 1) * P], w[:, :],
                                       start=True, stop=True)
                mm.then_inc(y_done, 1)

            def pair(m, k):
                pe.wait_ge(masked, m.n * NK + k + 1)
                b = (m.slot * NK + k) % XM
                for side in range(2):
                    mm = pe.matmul(th_ps[side * D:(side + 1) * D, :], w_pair[:, k, :], xm[:, b, side, :],
                                   start=(k == 0), stop=(k == NK - 1 and side == 0), skip_group_check=True)
                mm.then_inc(pair_done, 1)

            def add_edges(m):
                pe.wait_ge(e_staged[m.slot], (m.turn + 1) * DMA)
                for j in range(TG):
                    mm = pe.matmul(th_ps[D:P, j * P:(j + 1) * P], e_r[:, m.slot, j, :], ident[:, :],
                                   start=False, stop=(j == TG - 1), skip_group_check=True)
                mm.then_inc(main_done, 1)

            def scores(a):
                pe.wait_ge(prod_done, a.n + 1)
                wait(pe, delta_done, a.n - 1)
                for j in range(TG):
                    mm = pe.matmul(att_ps[:, (a.slot % 2) * TG + j:(a.slot % 2) * TG + j + 1],
                                   prod[:, a.slot % 2, j * P:(j + 1) * P], ones[0:D, :], start=True, stop=True)
                mm.then_inc(att_done, 1)

            def step(g):
                if live(g):
                    turn_in(g)
                    dense_turn(g)
                for k in range(NK):
                    if live(g, 1):
                        if k == 0:
                            wait(pe, prod_done, g.n - 1)
                        pair(g.back(1), k)
                    if k == 2 and live(g):
                        dense_y(g)
                    if k == 1 and live(g, 2):
                        scores(g.back(2))
                if live(g, 1):
                    add_edges(g.back(1))
            run_groups(pe, step, NG, 2)

            pe.wait_ge(max_done, NG)
            pe.matmul(typ_ps[:, 0:P], m_all[:, T:T + 1].to_broadcast([P, P]), ident[:, :], start=True, stop=True)
            pe.matmul(typ_ps[:, P:2 * P], dst_f[:, T - 1:T].to_broadcast([P, P]), ident[:, :],
                      start=True, stop=True).then_inc(ex_pe, 1)
            pe.wait_ge(ex_v, 6)
            pe.transpose(typ_ps[:, 2 * P:3 * P], mats[:, 3, :], ident[:, :]).then_inc(ex_pe, 1)
            pe.wait_ge(ex_v, 7)
            pe.wait_ge(sum_step, NG * TG)
            pe.wait_ge(den_done, NG)
            pe.matmul(att_ps[:, P:P + D], mats[:, 4, :], es_all[:, T, :], start=True, stop=True)
            pe.matmul(att_ps[:, P + D:P + D + 1], mats[:, 4, :], s_all[:, T:T + 1], start=True, stop=True).then_inc(ex_pe, 1)

            def final(g):
                b = g.slot % 2
                pe.wait_ge(uw_done, g.n + 1)
                wait(pe, uwT_out, g.n - 1)
                for j in range(TG):
                    mm = pe.transpose(xT_ps[:, b, j * P:(j + 1) * P], xm[:, b, 0, j * P:(j + 1) * P], ident[:, :])
                mm.then_inc(uwT_done, 1)
                pe.wait_ge(uwT_out, g.n + 1)
                wait(pe, z3_done, g.n - 1)
                for j in range(TG):
                    uwT = xm[:, b, 1, j * P:(j + 1) * P]
                    pe.matmul([th_ps, dT_ps][b][:, j * P:(j + 1) * P], uwT, bd_both[:, :], start=True, stop=True)
                    mm = pe.matmul(y_ps[:, b, j * D:(j + 1) * D], uwT, st_mix[:, :], start=True, stop=True)
                mm.then_inc(y3_done, 1)
            run_groups(pe, final, NG, 0)

        @block.scalar
        def _(act):
            act.wait_ge(setup_v, SETUP_V)

            def step(g):
                if live(g):
                    act.wait_ge(gathered[g.slot], (g.turn + 1) * 2 * TG * DMA)
                    act.copy(x_r[:, g.slot, :, :, 1, :], x_r[:, g.slot, :, :, 0, :]).then_inc(twice, 1)
                    act.wait_ge(dT_done, g.n + 1)
                    wait(act, y_done, g.n - 1)
                    act.copy(dT[:, g.slot % 2, :], dT_ps[:, :]).then_inc(dT_out, 1)
                    for side in range(2):
                        act.wait_ge(xT_done, 2 * g.n + side + 1)
                        if side == 0:
                            wait(act, masked, (g.n - 1) * NK)
                        act.copy(xT[:, g.slot % 2, side, :], xT_ps[:, side, :]).then_inc(xT_out, 1)
                    act.wait_ge(typ_done, g.n + 1)
                    act.copy(typ[:, g.slot % 2, :], typ_ps[:, :]).then_inc(typ_out, 1)
                    act.dma_start(xd_all[:, bass.ds(g.n * TG, TG), :], x_r[:, g.slot, 1, :, 0, :]).then_inc(xd_saved[g.slot], DMA)
                if live(g, 2):
                    squares(g.back(2), DR)
                if live(g, 4):
                    d = g.back(4)
                    normalise(d, DR, z[:, d.slot, :], o[:, d.slot % 2, :])
                    act.wait_ge(norm_done, d.n + 1)
                    dense_dma(act, False, d, o[:, d.slot % 2, :], o_stored[d.slot % 2])
                if live(g):
                    act.wait_ge(y_done, g.n + 1)
                    wait(act, z_done, g.n - 1)
                    act.activation(relu[:, g.slot % 2, :], y_ps[:, 0, :], ACT.Relu, scale=1.0 - SLOPE).then_inc(relu_done, 1)
                if live(g, 1):
                    m = g.back(1)
                    act.wait_ge(main_done, m.n + 1)
                    wait(act, prod_done, m.n - 1)
                    act.activation(g_r[:, m.slot % 2, :], th_ps[D:P, :], ACT.Tanh).then_inc(tanh_done, 1)
                if live(g, 2):
                    a = g.back(2)
                    b = a.slot % 2
                    act.wait_ge(delta_done, a.n + 1)
                    wait(act, den_done, a.n - 1)
                    wait(act, sum_step, (a.n - 1) * TG)
                    act.activation(wd[:, b, :, :], delta[:, b, :, :], ACT.Exp).then_inc(exp_done, 1)
                    act.wait_ge(exp_done, a.n + 1)
                    for j in range(TG):
                        ins = act.activation(wx[:, b, j, :], x_r[:, a.slot, 0, j, 0, :], ACT.Copy, scale=wd[:, b, 0, j:j + 1])
                    ins.then_inc(wx_done, 1)

            def squares(d, rows):
                act.wait_ge(mean_done, d.n + 1)
                wait(act, ssq_done, d.n - 1)
                for j in range(rows):
                    ins = act.activation(junk[:, d.slot % 2, j * D:(j + 1) * D], z[:, d.slot, j * D:(j + 1) * D], ACT.Square,
                                         bias=nmean[:, d.slot, j:j + 1], accum_out=ssq[:, d.slot, j:j + 1])
                ins.then_inc(ssq_done, 1)

            def normalise(d, rows, zin, to):
                act.wait_ge(bias_done, d.n + 1)
                n = d.back(2)
                if not known(n.turn) or n.turn >= 0:
                    act.wait_ge(o_stored[d.slot % 2], (n.turn * 2 + n.slot // 2 + 1) * DMA)
                for j in range(rows):
                    ins = act.activation(to[:, j * D:(j + 1) * D], zin[:, j * D:(j + 1) * D], ACT.Identity,
                                         scale=rstd[:, d.slot, j:j + 1], bias=nbias[:, d.slot, j:j + 1])
                ins.then_inc(norm_done, 1)
            run_groups(act, step, NG, 4)
            for q in range(2):
                act.wait_ge(o_stored[q], (-(-(NG - q) // 2)) * DMA + (dense_dmas(Group(NG // RING, 0)) if q == (NG - 1) % 2 else 0))
            act.wait_ge(norm_done, NG)
            act.activation(prev[:, 7:8], nbias[:, 0, 0:1], ACT.Copy).then_inc(dense_stored, 1)
            act.wait_ge(ex_v, 5)
            act.activation(mats[:, 2, :], mats[:, 1, :], ACT.Exp, bias=prev[:, 1:2]).then_inc(ex_act, 1)
            act.wait_ge(ex_v, 13)
            act.activation(tab[:, 5 * T:7 * T], tab[:, 3 * T:5 * T], ACT.Exp).then_inc(ex_act, 1)

            def final(g):
                b = g.slot % 2
                if live(g):
                    act.wait_ge(uwT_done, g.n + 1)
                    wait(act, y3_done, g.n - 1)
                    act.copy(xm[:, b, 1, :], xT_ps[:, b, :]).then_inc(uwT_out, 1)
                if live(g, 1):
                    d = g.back(1)
                    act.wait_ge(mean3_done, d.n + 1)
                    wait(act, sq3_done, d.n - 1)
                    for j in range(TG):
                        ins = act.activation(junk[:, d.slot % 2, j * D:(j + 1) * D], z[:, d.slot, j * D:(j + 1) * D], ACT.Square,
                                             bias=nmean[:, d.slot, j:j + 1], accum_out=ssq[:, d.slot, j:j + 1])
                    ins.then_inc(sq3_done, 1)
                if live(g, 2):
                    d = g.back(2)
                    act.wait_ge(var3_done, d.n + 1)
                    act.activation(rstd[:, d.slot, 0:TG], var[:, d.slot, 0:TG], ACT.Sqrt).then_inc(sqrt3_done, 1)
                if live(g, 3):
                    d = g.back(3)
                    act.wait_ge(bias3_done, d.n + 1)
                    wait(act, scattered[d.slot], d.turn * TG * DMA)
                    for j in range(TG):
                        ins = act.activation(out_r[:, d.slot, j, :], z[:, d.slot, j * D:(j + 1) * D], ACT.Identity,
                                             scale=var[:, d.slot, j:j + 1], bias=nbias[:, d.slot, j:j + 1])
                    ins.then_inc(norm3_done, 1)
                if live(g):
                    act.wait_ge(y3_done, g.n + 1)
                    wait(act, z3_done, g.n - 1)
                    act.activation(relu[:, b, :], [th_ps, dT_ps][b][:, :], ACT.Relu, scale=1.0 - SLOPE).then_inc(relu3_done, 1)
            run_groups(act, final, NG, 3)

        @block.vector
        def _(v):
            v.memset(ends_i[96:P, :, LASTC:T], 0).then_inc(tables_zero, 1)
            v.memset(type_i[96:P, LASTC:T], 0).then_inc(tables_zero, 1)
            v.memset(next_i[:, :], FAR).then_inc(tables_zero, 1)
            v.memset(es_all[96:P, LASTC + 1:T + 1, :], 0.0).then_inc(e_zero, 1)
            v.wait_ge(tables_in, 11 * DMA)
            v.tensor_copy(dst_f0[:, 0:T], ends_i[:, 1, :]).then_inc(setup_v, 1)
            v.tensor_copy(dst_f0[:, T:T + 1], next_i[:, 0:1]).then_inc(setup_v, 1)
            v.tensor_copy(type_b[:, :], type_i[:, :]).then_inc(setup_v, 1)
            v.memset(m_all[:, 0:1], 0.0).then_inc(setup_v, 1)
            v.memset(s_all[:, 0:1], 0.0).then_inc(setup_v, 1)
            v.memset(es_all[:, 0, :], 0.0).then_inc(setup_v, 1)
            v.memset(bd_res[:, :], 0.0).then_inc(setup_v, 1)
            v.memset(bd_both[:, :], 0.0).then_inc(setup_v, 1)
            v.wait_ge(consts, 7)
            v.tensor_copy(identb[:, :], ident[:, :]).then_inc(setup_v, 1)
            v.tensor_copy(relk[0:D, :], relk0[0:D, :]).then_inc(setup_v, 1)
            v.tensor_scalar(relk[D:P, :], relk0[D:P, :], 1.0, None, ALU.add).then_inc(setup_v, 1)
            v.wait_ge(resT, 1)
            v.wait_ge(setup_v, 8)
            for h in range(2):
                q = slice(h * D, (h + 1) * D)
                v.tensor_copy(bd_res[q, q], att_ps[q, 0:D]).then_inc(setup_v, 1)
                v.tensor_copy(bd_both[q, q], att_ps[q, D:2 * D]).then_inc(setup_v, 1)
            v.tensor_scalar(st_mix[:, :], att_ps[:, D:2 * D], SLOPE, None, ALU.mult).then_inc(setup_v, 1)
            v.wait_ge(setup_v, 15)
            v.scalar_tensor_tensor(bd_mix[:, :], bd_res[:, :], SLOPE, ident[:, :], ALU.mult, ALU.add).then_inc(setup_v, 1)
            v.wait_ge(dst_masked, 1)
            v.tensor_tensor(same[:, :], dst_f[:, 0:T], dst_f[:, 1:T + 1], ALU.is_equal).then_inc(setup_v, 1)
            v.tensor_scalar(inf_f[:, :], dst_f[:, 0:T], dst_f[:, 0:1], None, ALU.is_equal).then_inc(setup_v, 1)
            v.wait_ge(setup_v, 18)
            v.memset(start[:, 0:1], -BIG).then_inc(setup_v, 1)
            v.tensor_scalar(start[:, 1:T], same[:, 0:T - 1], -1.0, BIG, ALU.add, ALU.mult).then_inc(setup_v, 1)
            v.scalar_tensor_tensor(row_i[:, :], same[:, :], float(FAR), dst_f[:, 0:T], ALU.mult, ALU.add).then_inc(setup_v, 1)
            v.wait_ge(setup_v, SETUP_V)

            def mask(m, k):
                if k == 0:
                    v.wait_ge(xT_out, 2 * m.n + 2)
                    v.wait_ge(typ_out, m.n + 1)
                wait(v, pair_done, m.n * NK + k + 1 - XM)
                b = (m.slot * NK + k) % XM
                v.scalar_tensor_tensor(xm[:, b, :, :], typ[:, m.slot % 2, :].unsqueeze(1).to_broadcast([P, 2, W]),
                                       relk[:, k:k + 1], xT[:, m.slot % 2, :, :], ALU.is_equal, ALU.mult).then_inc(masked, 1)

            def guess(d):
                bits = newt[:, 0, :].bitcast(I32)
                wait(v, newt_step, d.n * 11)
                v.wait_ge(var_done, d.n + 1)
                v.tensor_scalar(bits, var[:, d.slot, :].bitcast(I32), 1, None, ALU.logical_shift_right).then_inc(newt_step, 1)
                v.wait_ge(newt_step, d.n * 11 + 1)
                wait(v, norm_done, d.n - RING + 1)
                v.tensor_scalar(rstd[:, d.slot, :].bitcast(I32), bits, -1.0, float(MAGIC), ALU.mult, ALU.add).then_inc(newt_step, 1)

            def refine(d, n):
                y, v_, a, b = rstd[:, d.slot, :], var[:, d.slot, :], newt[:, 0, :], newt[:, 1, :]
                at = d.n * 11 + 2 + 3 * n
                v.wait_ge(newt_step, at)
                v.tensor_tensor(a, y, y, ALU.mult).then_inc(newt_step, 1)
                v.wait_ge(newt_step, at + 1)
                v.scalar_tensor_tensor(b, a, -0.5, v_, ALU.mult, ALU.mult).then_inc(newt_step, 1)
                v.wait_ge(newt_step, at + 2)
                v.scalar_tensor_tensor(y, b, 1.5, y, ALU.add, ALU.mult).then_inc(newt_step, 1)

            def sum_one(s, j):
                v.wait_ge(wx_done, s.n + 1)
                wait(v, sum_step, s.n * TG + j)
                c = s.n * TG + j
                v.scalar_tensor_tensor(es_all[:, bass.ds(c + 1, 1), :].rearrange("p a f -> p (a f)"),
                                       es_all[:, bass.ds(c, 1), :].rearrange("p a f -> p (a f)"),
                                       wd[:, s.slot % 2, 1, j:j + 1], wx[:, s.slot % 2, j, :],
                                       ALU.mult, ALU.add).then_inc(sum_step, 1)

            def step(g):
                m, a, s, d, dv, dn = g.back(1), g.back(2), g.back(3), g.back(1), g.back(2), g.back(3)
                if live(g, 1):
                    mask(m, 0)
                if live(g, 2):
                    v.wait_ge(tanh_done, a.n + 1)
                    wait(v, att_done, a.n - 1)
                    v.tensor_tensor(prod[:, a.slot % 2, :], th_ps[0:D, :], g_r[:, a.slot % 2, :],
                                    ALU.mult).then_inc(prod_done, 1)
                if live(g, 3):
                    sum_one(s, 0)
                    guess(dn)
                if live(g, 1):
                    mask(m, 1)
                if live(g, 3):
                    sum_one(s, 1)
                    refine(dn, 0)
                if live(g, 1):
                    mask(m, 2)
                    wait(v, norm_done, d.n - RING + 1)
                    v.wait_ge(relu_done, d.n + 1)
                    v.tensor_tensor(z[:, d.slot, :], relu[:, d.slot % 2, :], y_ps[:, 1, :], ALU.add).then_inc(z_done, 1)
                if live(g, 3):
                    sum_one(s, 2)
                    refine(dn, 1)
                if live(g, 2):
                    v.wait_ge(att_done, a.n + 1)
                    wait(v, max_done, a.n)
                    col = bass.ds(a.n * TG + 1, TG)
                    att = att_ps[:, (a.slot % 2) * TG:(a.slot % 2) * TG + TG]
                    v.tensor_tensor_scan(m_all[:, col], start[:, bass.ds(a.n * TG, TG)], att,
                                         m_all[:, bass.ds(a.n * TG, 1)], ALU.add, ALU.max).then_inc(max_done, 1)
                if live(g, 1):
                    mask(m, 3)
                    v.wait_ge(z_done, d.n + 1)
                    v.tensor_reduce(zsum[:, d.slot, :], z[:, d.slot, :].rearrange("p (j f) -> p j f", f=D), AX.X,
                                    ALU.add).then_inc(zsum_done, 1)
                if live(g, 3):
                    sum_one(s, 3)
                    refine(dn, 2)
                if live(g, 2):
                    b = a.slot % 2
                    v.wait_ge(max_done, a.n + 1)
                    wait(v, exp_done, a.n - 1)
                    v.tensor_tensor(delta[:, b, 0, :], att, m_all[:, col], ALU.subtract)
                    v.tensor_tensor(delta[:, b, 1, :], m_all[:, bass.ds(a.n * TG, TG)], m_all[:, col],
                                    ALU.subtract).then_inc(sub_done, 1)
                if live(g, 1):
                    mask(m, 4)
                    v.wait_ge(zsum_done, d.n + 1)
                    v.tensor_scalar(nmean[:, d.slot, :], zsum[:, d.slot, :], -1.0 / D, None, ALU.mult).then_inc(mean_done, 1)
                if live(g, 2):
                    v.wait_ge(sub_done, a.n + 1)
                    v.tensor_tensor(delta[:, b, 1, :], delta[:, b, 1, :], start[:, bass.ds(a.n * TG, TG)],
                                    ALU.add).then_inc(delta_done, 1)
                    v.wait_ge(ssq_done, dv.n + 1)
                    v.tensor_scalar(var[:, dv.slot, :], ssq[:, dv.slot, :], 1.0 / D, EPS, ALU.mult, ALU.add).then_inc(var_done, 1)
                if live(g, 3):
                    sb_ = s.slot % 2
                    v.wait_ge(newt_step, dn.n * 11 + 11)
                    v.tensor_tensor(nbias[:, dn.slot, :], nmean[:, dn.slot, :], rstd[:, dn.slot, :], ALU.mult).then_inc(bias_done, 1)
                    wait(v, den_done, s.n)
                    v.tensor_tensor_scan(s_all[:, bass.ds(s.n * TG + 1, TG)], wd[:, sb_, 1, :], wd[:, sb_, 0, :],
                                         s_all[:, bass.ds(s.n * TG, 1)], ALU.mult, ALU.add).then_inc(den_done, 1)
            run_groups(v, step, NG, 3)

            msk, aa = mats[:, 0, :], mats[:, 1, :]
            v.wait_ge(ex_pe, 1)
            v.scalar_tensor_tensor(msk, typ_ps[:, P:2 * P], dst_f[:, 0:1], before[:, :], ALU.is_equal, ALU.mult).then_inc(ex_v, 1)
            v.wait_ge(ex_v, 1)
            v.tensor_tensor(aa, typ_ps[:, 0:P], msk, ALU.mult).then_inc(ex_v, 1)
            v.tensor_scalar(mats[:, 2, :], msk, -1.0, NONE, ALU.add, ALU.mult).then_inc(ex_w, 1)
            v.wait_ge(ex_v, 2)
            v.wait_ge(ex_w, 1)
            v.tensor_tensor(aa, aa, mats[:, 2, :], ALU.add).then_inc(ex_v, 1)
            v.wait_ge(ex_v, 3)
            v.tensor_reduce(prev[:, 0:1], aa, AX.X, ALU.max).then_inc(ex_v, 1)
            v.wait_ge(ex_v, 4)
            v.tensor_scalar(prev[:, 1:2], prev[:, 0:1], -1.0, None, ALU.mult).then_inc(ex_v, 1)
            v.wait_ge(ex_act, 1)
            v.tensor_tensor(mats[:, 3, :], mats[:, 2, :], msk, ALU.mult).then_inc(ex_v, 1)
            v.wait_ge(ex_pe, 2)
            v.tensor_copy(mats[:, 4, :], typ_ps[:, 2 * P:3 * P]).then_inc(ex_v, 1)
            t2, mm, da, db, ea, eb = (tab[:, k * T:(k + 1) * T] for k in (2, 7, 3, 4, 5, 6))
            own, den = tab[:, 8 * T:9 * T], tab[:, 9 * T:10 * T]
            v.wait_ge(z_done, NG)
            v.tensor_scalar(t2, inf_f[:, :], -1.0, NONE, ALU.add, ALU.mult).then_inc(ex_v, 1)
            v.wait_ge(ex_v, 8)
            v.scalar_tensor_tensor(own, inf_f[:, :], prev[:, 0:1], t2, ALU.mult, ALU.add).then_inc(ex_v, 1)
            v.wait_ge(ex_v, 9)
            v.tensor_tensor(mm, m_all[:, 1:T + 1], own, ALU.max).then_inc(ex_v, 1)
            v.wait_ge(ex_v, 10)
            v.tensor_tensor(da, m_all[:, 1:T + 1], mm, ALU.subtract).then_inc(ex_v, 1)
            v.tensor_tensor(db, own, mm, ALU.subtract).then_inc(ex_v, 1)
            v.wait_ge(ex_pe, 3)
            v.tensor_copy(carry[:, :], att_ps[:, P:P + D + 1]).then_inc(ex_v, 1)
            v.wait_ge(ex_v, 13)
            v.wait_ge(ex_act, 2)
            v.tensor_tensor(own, ea, s_all[:, 1:T + 1], ALU.mult).then_inc(ex_v, 1)
            v.wait_ge(ex_v, 14)
            v.scalar_tensor_tensor(den, eb, carry[:, D:D + 1], own, ALU.mult, ALU.add).then_inc(ex_v, 1)
            v.wait_ge(ex_v, 15)
            v.reciprocal(mm, den).then_inc(ex_v, 1)
            v.wait_ge(ex_v, 16)
            v.tensor_tensor(fa, ea, mm, ALU.mult).then_inc(ex_v, 1)
            v.tensor_tensor(fb, eb, mm, ALU.mult).then_inc(ex_v, 1)
            v.wait_ge(ex_v, 18)

            def final(g):
                b = g.slot % 2
                if live(g, 2):
                    d = g.back(2)
                    v.wait_ge(sq3_done, d.n + 1)
                    v.tensor_scalar(var[:, d.slot, 0:TG], ssq[:, d.slot, 0:TG], 1.0 / D, EPS, ALU.mult, ALU.add).then_inc(var3_done, 1)
                if live(g):
                    cols = bass.ds(g.n * TG, TG)
                    own_, car, h = (xT[:, b, k // 2, (k % 2) * 256:(k % 2) * 256 + 256].rearrange("p (j f) -> p j f", f=D)
                                    for k in range(3))
                    uw = xm[:, b, 0, :].rearrange("p (j k f) -> p j k f", k=2, f=D)
                    xd = xd_all[:, cols, :]
                    wait(v, scattered[g.slot], g.turn * TG * DMA)
                    v.tensor_copy(row_r[:, g.slot, :], row_i[:, cols]).then_inc(row_done, 1)
                    wait(v, h_step, (g.n - 1) * 3)
                    v.tensor_tensor(own_, es_all[:, bass.ds(g.n * TG + 1, TG), :],
                                    fa[:, cols].unsqueeze(2).to_broadcast([P, TG, D]), ALU.mult).then_inc(h_step, 1)
                    v.tensor_tensor(car, carry[:, 0:D].unsqueeze(1).to_broadcast([P, TG, D]),
                                    fb[:, cols].unsqueeze(2).to_broadcast([P, TG, D]), ALU.mult).then_inc(h_step, 1)
                if live(g, 3):
                    d = g.back(3)
                    v.wait_ge(sqrt3_done, d.n + 1)
                    v.reciprocal(var[:, d.slot, 0:TG], rstd[:, d.slot, 0:TG]).then_inc(rec3_done, 1)
                if live(g):
                    v.wait_ge(h_step, g.n * 3 + 2)
                    v.tensor_tensor(h, own_, car, ALU.add).then_inc(h_step, 1)
                if live(g, 3):
                    v.wait_ge(rec3_done, d.n + 1)
                    v.tensor_tensor(nbias[:, d.slot, 0:TG], nmean[:, d.slot, 0:TG], var[:, d.slot, 0:TG],
                                    ALU.mult).then_inc(bias3_done, 1)
                if live(g):
                    v.wait_ge(h_step, g.n * 3 + 3)
                    wait(v, uwT_done, g.n - 1)
                    v.tensor_tensor(uw[:, :, 0, :], h, xd, ALU.add)
                    v.tensor_tensor(uw[:, :, 1, :], h, xd, ALU.mult).then_inc(uw_done, 1)
                if live(g, 1):
                    d = g.back(1)
                    c = d.slot % 2
                    r2 = relu[:, c, :].rearrange("p (j k f) -> p j k f", k=2, f=D)
                    za, zb = (prod_ex[:, c, k, :] for k in range(2))
                    v.wait_ge(relu3_done, d.n + 1)
                    wait(v, z3_done, d.n - 1)
                    v.tensor_tensor(za.rearrange("p (j f) -> p j f", f=D), r2[:, :, 0, :], r2[:, :, 1, :], ALU.add).then_inc(za_done, 1)
                    v.tensor_tensor(zb.rearrange("p (j f) -> p j f", f=D),
                                    y_ps[:, c, 0:TG * D].rearrange("p (j f) -> p j f", f=D),
                                    xd_all[:, bass.ds(d.n * TG, TG), :], ALU.add).then_inc(za_done, 1)
                    v.wait_ge(za_done, 2 * d.n + 2)
                    wait(v, norm3_done, d.n - RING + 1)
                    v.tensor_tensor(z[:, d.slot, 0:TG * D], za, zb, ALU.add).then_inc(z3_done, 1)
                    v.wait_ge(z3_done, d.n + 1)
                    v.tensor_reduce(zsum[:, d.slot, 0:TG], z[:, d.slot, 0:TG * D].rearrange("p (j f) -> p j f", f=D), AX.X,
                                    ALU.add).then_inc(zsum3_done, 1)
                    v.wait_ge(zsum3_done, d.n + 1)
                    v.tensor_scalar(nmean[:, d.slot, 0:TG], zsum[:, d.slot, 0:TG], -1.0 / D, None, ALU.mult).then_inc(mean3_done, 1)
            run_groups(v, final, NG, 3)


def kernel(**inputs):
    import numpy as np
    import concourse.bacc as bacc
    from concourse.bass_utils import run_bass_kernel_spmd

    nc = bacc.Bacc("TRN2", target_bir_lowering=False, num_devices=1)
    arrays, args = {}, []
    for name in ["x", "src", "dst", "edge_attr_64", "edge_type_10", "L0_gnn_relation_weight", "L0_gnn_res_fc_w",
                 "L0_gnn_res_fc2_w"]:
        a = np.ascontiguousarray(inputs[name])
        arrays[f"in_{name}"] = a
        args.append(nc.dram_tensor(f"in_{name}", a.shape, mybir.dt.from_np(a.dtype), kind="ExternalInput").ap())
    args.append(nc.dram_tensor("out", inputs["x"].shape, F32, kind="ExternalOutput").ap())
    gnn_resnorm(nc, *args)
    return run_bass_kernel_spmd(nc, [arrays], core_ids=[0]).results[0]["out"]
```

```python
from contextlib import ExitStack

import concourse.bass as bass
from concourse import mybir

ALU = mybir.AluOpType
ACT = mybir.ActivationFunctionType
AX = mybir.AxisListType
F32 = mybir.dt.float32
BF16 = mybir.dt.bfloat16
I32 = mybir.dt.int32

P = 128
DMA = 16
TG = 4
RING = 4
BIG = 3.0e38
NONE = 1.0e30
FAR = 1 << 20
SLOPE = 0.01
EPS = 1e-5
MAGIC = 0x5F3759DF
XM = 4


class Group:

    def __init__(self, turn, slot):
        self.turn, self.slot = turn, slot
        self.n = turn * RING + slot

    def back(self, k):
        turn, slot = self.turn, self.slot - k
        while slot < 0:
            turn, slot = turn - 1, slot + RING
        return Group(turn, slot)


def known(v):
    return isinstance(v, int)


def wait(eng, sem, value):
    if not known(value) or value > 0:
        eng.wait_ge(sem, value)


def hold(pool, tile, done, g):
    wait(pool, done, g.n - RING + 1)
    pool.tensor_tensor(tile[:, g.slot + 1:g.slot + 2], tile[:, 0:1], tile[:, 0:1], ALU.add).then_inc(done, 1)


def run_groups(eng, step, groups, lag, first=None):
    if first is None:
        first = 1 if lag == 0 else 2
    last = groups // RING
    for it in range(first * RING):
        step(Group(it // RING, it % RING))
    with eng.Fori(first, last) as turn:
        for slot in range(RING):
            step(Group(turn, slot))
    for it in range(last * RING, groups + lag):
        step(Group(it // RING, it % RING))


def gnn_resnorm(nc, x, src, dst, eattr, etype, relw, resw, resw2, out):
    N, D = x.shape
    E = src.shape[0]
    R = relw.shape[0]
    T = -(-E // P)
    NG = T // TG
    assert T % TG == 0 and D == 64 and R % 2 == 0
    NK = R // 2
    LASTC = E - (P - 1) * T
    W = TG * P
    DR = -(-N // (NG * P))
    DB = P * DR
    DLAST = N - (NG - 1) * DB
    assert DR % 2 == 0 and DR * D == 512 and DLAST % DR == 0 and 0 < LASTC < T
    PL = DLAST // DR
    PL0 = PL // DMA * DMA

    with ExitStack() as ctx:
        def sb(name, shape, dt=F32):
            return ctx.enter_context(nc.sbuf_tensor(name, shape, dt))

        def ps(name, shape):
            return ctx.enter_context(nc.psum_tensor(name, shape, F32))

        def sem(name):
            return ctx.enter_context(nc.semaphore(name))

        ident = sb("ident", [P, P])
        identb = sb("identb", [P, P], BF16)
        ones = sb("ones", [P, 1])
        relk0 = sb("relk0", [P, NK])
        relk = sb("relk", [P, NK])
        before = sb("before", [P, P])
        w_pair = sb("w_pair", [P, NK, D])
        res_rows = sb("res_rows", [D, 3 * D])
        bd_res = sb("bd_res", [P, P])
        bd_mix = sb("bd_mix", [P, P])
        bd_both = sb("bd_both", [P, P])
        st_mix = sb("st_mix", [P, D])
        ends_i = sb("ends_i", [P, 2, T], I32)
        next_i = sb("next_i", [P, 2], I32)
        type_i = sb("type_i", [P, T], I32)
        type_b = sb("type_b", [P, T], BF16)
        dst_f0 = sb("dst_f0", [P, T + 1])
        dst_f = sb("dst_f", [P, T + 1])
        same = sb("same", [P, T])
        start = sb("start", [P, T])
        row_i = sb("row_i", [P, T], I32)
        inf_f = sb("inf_f", [P, T])
        m_all = sb("m_all", [P, T + 1])
        s_all = sb("s_all", [P, T + 1])
        es_all = sb("es_all", [P, T + 1, D])
        xd_all = sb("xd_all", [P, T, D])
        idx = sb("idx", [P, RING, 2, TG], I32)
        x_r = sb("x_r", [P, RING, 2, TG, 2, D])
        e_r = sb("e_r", [P, RING, TG, D])
        xT = sb("xT", [P, 2, 2, W])
        typ = sb("typ", [P, 2, W])
        xm = sb("xm", [P, XM, 2, W])
        g_r = sb("g_r", [D, 2, W])
        prod = sb("prod", [D, 2, W])
        delta = sb("delta", [P, 2, 2, TG])
        wd = sb("wd", [P, 2, 2, TG])
        wx = sb("wx", [P, 2, TG, D])
        x_in = sb("x_in", [P, RING, DR * D])
        dT = sb("dT", [P, 2, 512])
        relu = sb("relu", [P, 2, 512])
        z = sb("z", [P, RING, DR * D])
        o = sb("o", [P, 2, DR * D])
        junk = sb("junk", [P, 2, DR * D])
        held = sb("held", [P, 2, RING + 1])
        newt = sb("newt", [P, 2, DR])
        row_r = sb("row_r", [P, RING, TG], I32)
        out_r = sb("out_r", [P, RING, TG, D])
        prev = sb("prev", [P, 8])
        carry = sb("carry", [P, D + 1])
        zsum = sb("zsum", [P, RING, DR])
        nmean = sb("nmean", [P, RING, DR])
        ssq = sb("ssq", [P, RING, DR])
        var = sb("var", [P, RING, DR])
        rstd = sb("rstd", [P, RING, DR])
        nbias = sb("nbias", [P, RING, DR])

        xT_ps = ps("xT_ps", [P, 2, W])
        typ_ps = ps("typ_ps", [P, W])
        th_ps = ps("th_ps", [P, W])
        att_ps = ps("att_ps", [P, 512])
        dT_ps = ps("dT_ps", [P, 512])
        y_ps = ps("y_ps", [P, 2, 512])

        tab = x_in.rearrange("p a b -> p (a b)")
        mats = e_r.rearrange("p a b f -> p (a b f)")[:, 0:5 * P].rearrange("p (k q) -> p k q", q=P)
        prod_ex = o.rearrange("p a (k f) -> p a k f", k=2)
        fa, fb = tab[:, 0:T], tab[:, T:2 * T]

        tables_zero, tables_in, w_in, e_in = sem("tables_zero"), sem("tables_in"), sem("w_in"), [sem("e_in0"), sem("e_in1")]
        edges_in, twice, sub_done, e_zero = sem("edges_in"), sem("twice"), sem("sub_done"), sem("e_zero")
        consts, dst_masked = sem("consts"), sem("dst_masked")
        setup_v, resT = sem("setup_v"), sem("resT")
        idx_in = [sem(f"idx_in{i}") for i in range(RING)]
        e_staged = [sem(f"e_staged{i}") for i in range(RING)]
        gathered = [sem(f"gathered{i}") for i in range(RING)]
        xd_saved = [sem(f"xd_saved{i}") for i in range(RING)]
        x_loaded = [sem(f"x_loaded{i}") for i in range(RING)]
        o_stored = [sem(f"o_stored{i}") for i in range(2)]
        xT_done, xT_out, typ_done, typ_out = sem("xT_done"), sem("xT_out"), sem("typ_done"), sem("typ_out")
        masked, pair_done = sem("masked"), sem("pair_done")
        tanh_done, prod_done, att_done, max_done = sem("tanh_done"), sem("prod_done"), sem("att_done"), sem("max_done")
        delta_done, exp_done, wx_done, sum_step, den_done = (
            sem("delta_done"), sem("exp_done"), sem("wx_done"), sem("sum_step"), sem("den_done"))
        dT_done, dT_out, y_done, relu_done, z_done = (
            sem("dT_done"), sem("dT_out"), sem("y_done"), sem("relu_done"), sem("z_done"))
        held_gather, held_scatter = sem("held_gather"), sem("held_scatter")
        newt_step, dense_stored = sem("newt_step"), sem("dense_stored")
        ex_pe, ex_v, ex_w, ex_act = sem("ex_pe"), sem("ex_v"), sem("ex_w"), sem("ex_act")
        scattered = [sem(f"scattered{i}") for i in range(RING)]
        row_done, h_step, uw_done, uwT_done, uwT_out, y3_done, relu3_done, za_done, z3_done, zsum3_done = (
            sem(n) for n in ["row_done", "h_step", "uw_done", "uwT_done", "uwT_out", "y3_done", "relu3_done", "za_done",
                             "z3_done", "zsum3_done"])
        mean3_done, sq3_done, var3_done, sqrt3_done, rec3_done, bias3_done, norm3_done = (
            sem(n) for n in ["mean3_done", "sq3_done", "var3_done", "sqrt3_done", "rec3_done", "bias3_done", "norm3_done"])
        zsum_done, mean_done, ssq_done, var_done, rstd_done, bias_done, norm_done = (
            sem("zsum_done"), sem("mean_done"), sem("ssq_done"), sem("var_done"), sem("rstd_done"),
            sem("bias_done"), sem("norm_done"))

        SETUP_V = 22
        E0 = 8 * TG

        def live(g, k=0):
            return not known(g.turn) or 0 <= g.n - k < NG

        def x_block(d, part=slice(0, P)):
            return x[bass.ds(d.n * DB, DB), :].rearrange("(p j) f -> p (j f)", j=DR)

        def dense_dma(eng, to_sbuf, d, tile, done):
            dram = x if to_sbuf else out
            if known(d.turn) and d.n == NG - 1:
                parts = [(0, PL0), (PL0, PL)] if PL0 < PL else [(0, PL)]
            else:
                parts = [(0, P)]
            for a, b in parts:
                rows = dram[bass.ds(d.n * DB + a * DR, (b - a) * DR), :].rearrange("(p j) f -> p (j f)", j=DR)
                if to_sbuf:
                    eng.dma_start(tile[a:b, :], rows).then_inc(done, DMA)
                else:
                    eng.dma_start(rows, tile[a:b, :]).then_inc(done, DMA)

        def dense_dmas(d):
            return DMA if known(d.turn) and d.n == NG - 1 and PL0 < PL else 0

        ctx2 = ctx.enter_context(nc.Block())
        block = ctx2

        @block.sync
        def _(sp):
            def table(dram, tile):
                rows = dram[0:(P - 1) * T].rearrange("(p c) -> p c", c=T)
                a = (P - 1) // DMA * DMA
                sp.dma_start(tile[0:a, 0:T], rows[0:a, :]).then_inc(tables_in, DMA)
                sp.dma_start(tile[a:P - 1, 0:T], rows[a:P - 1, :]).then_inc(tables_in, DMA)
                sp.dma_start(tile[P - 1:P, 0:LASTC], dram[(P - 1) * T:E].rearrange("(a c) -> a c", a=1)).then_inc(tables_in, DMA)
            sp.wait_ge(tables_zero, 3)
            table(src, ends_i[:, 0, :])
            table(dst, ends_i[:, 1, :])
            table(etype, type_i[:, :])
            heads = dst[T:(P - 1) * T].rearrange("(p c) -> p c", c=T)
            sp.dma_start(next_i[0:P - 2, :], heads[:, 0:2]).then_inc(tables_in, DMA)
            sp.dma_start(next_i[P - 2:P - 1, :], dst[(P - 1) * T:(P - 1) * T + 2].rearrange("(a c) -> a c", a=1)).then_inc(tables_in, DMA)
            for h in range(2):
                sp.dma_start(w_pair[h * D:(h + 1) * D, :, :],
                             relw.rearrange("(k h) i o -> h i k o", h=2)[h]).then_inc(w_in, DMA)
            for n, w in enumerate([resw, resw, resw2]):
                sp.dma_start(res_rows[:, n * D:(n + 1) * D], w[:, :]).then_inc(w_in, DMA)
            rows = eattr[0:(P - 1) * T, :].rearrange("(p c) f -> p c f", c=T)
            a = (P - 1) // DMA * DMA
            last = eattr[(P - 1) * T:E, :].rearrange("(a c) f -> a c f", a=1)
            sp.wait_ge(e_zero, 1)
            for n, (c0, c1) in enumerate([(0, E0), (E0, T)]):
                c2 = min(c1, LASTC)
                sp.dma_start(es_all[0:a, c0 + 1:c1 + 1, :], rows[0:a, c0:c1, :]).then_inc(e_in[n], DMA)
                sp.dma_start(es_all[a:P - 1, c0 + 1:c1 + 1, :], rows[a:P - 1, c0:c1, :]).then_inc(e_in[n], DMA)
                sp.dma_start(es_all[P - 1:P, c0 + 1:c2 + 1, :], last[:, c0:c2, :]).then_inc(e_in[n], DMA)
            sp.wait_ge(tables_in, 11 * DMA)

            def step(g):
                if live(g):
                    wait(sp, gathered[g.slot], g.turn * 2 * TG * DMA)
                    sp.dma_start(idx[:, g.slot, :, :], ends_i[:, :, bass.ds(g.n * TG, TG)]).then_inc(idx_in[g.slot], DMA)
                    wait(sp, z_done, g.n - RING + 1)
                    dense_dma(sp, True, g, x_in[:, g.slot, :], x_loaded[g.slot])
                    if known(g.turn) and g.n in (0, 7):
                        sp.wait_ge(e_in[min(g.n, 1)], 3 * DMA)
                    wait(sp, edges_in, g.n - RING + 1)
                    sp.dma_start(e_r[:, g.slot, :, :], es_all[:, bass.ds(g.n * TG + 1, TG), :]).then_inc(e_staged[g.slot], DMA)
            run_groups(sp, step, NG, 0, first=2)

        @block.gpsimd
        def _(pool):
            pool.memset(ones[:, :], 1.0).then_inc(consts, 1)
            pool.memset(held[:, :, 0:1], 0.0).then_inc(consts, 1)
            pool.memset(ident[:, :], 0.0).then_inc(consts, 1)
            pool.memset(before[:, :], 1.0).then_inc(consts, 1)
            pool.iota(relk0[:, :], [[2, NK]], base=0, channel_multiplier=0,
                      allow_small_or_imprecise_dtypes=True).then_inc(consts, 1)
            pool.wait_ge(consts, 5)
            pool.affine_select(ident[:, :], ident[:, :], [[-1, P]], ALU.not_equal, 1.0, base=0,
                               channel_multiplier=1).then_inc(consts, 1)
            pool.affine_select(before[:, :], before[:, :], [[-1, P]], ALU.is_ge, 0.0, base=-1,
                               channel_multiplier=1).then_inc(consts, 1)

            def step(g):
                if live(g):
                    pool.wait_ge(idx_in[g.slot], (g.turn + 1) * DMA)
                    wait(pool, wx_done, g.n - RING + 1)
                    wait(pool, xd_saved[g.slot], g.turn * DMA)
                    hold(pool, held[:, 0, :], held_gather, g)
                if live(g):
                    for j in range(TG):
                        for side in range(2):
                            pool.indirect_dma_start(
                                x_r[:, g.slot, side, j, 0, :], None, x[:, :],
                                bass.IndirectOffsetOnAxis(ap=idx[:, g.slot, side, j:j + 1], axis=0),
                            ).then_inc(gathered[g.slot], DMA)
                if known(g.turn) and g.n == 0:
                    pool.wait_ge(setup_v, 2)
                    pool.affine_select(dst_f[:, :], dst_f0[:, :], [[-1, T + 1]], ALU.is_ge, float(FAR),
                                       base=E - 1, channel_multiplier=-T).then_inc(dst_masked, 1)
            run_groups(pool, step, NG, 0)

            def scatter(g):
                pool.wait_ge(row_done, g.n + 1)
                pool.wait_ge(norm3_done, g.n + 1)
                hold(pool, held[:, 1, :], held_scatter, g)
                for j in range(TG):
                    pool.indirect_dma_start(
                        out[:, :], bass.IndirectOffsetOnAxis(ap=row_r[:, g.slot, j:j + 1], axis=0),
                        out_r[:, g.slot, j, :], None, bounds_check=top, oob_is_err=False,
                    ).then_inc(scattered[g.slot], DMA)
            pool.wait_ge(dense_stored, 1)
            top = pool.to_reg(N - 1)
            run_groups(pool, scatter, NG, 0)
            for q in range(RING):
                pool.wait_ge(scattered[q], -(-(NG - q) // RING) * TG * DMA)

        @block.tensor
        def _(pe):
            pe.wait_ge(w_in, 5 * DMA)
            pe.wait_ge(consts, 7)
            pe.transpose(att_ps[:, 0:D], res_rows[:, 0:2 * D], ident[0:D, 0:D])
            pe.transpose(att_ps[:, D:2 * D], res_rows[:, D:3 * D], ident[0:D, 0:D]).then_inc(resT, 1)
            pe.wait_ge(setup_v, SETUP_V)

            def turn_in(g):
                pe.wait_ge(twice, g.n + 1)
                wait(pe, xT_out, 2 * g.n)
                for side in range(2):
                    for j in range(TG):
                        mm = pe.transpose(xT_ps[:, side, j * P:(j + 1) * P],
                                          x_r[:, g.slot, side, j, :, :].rearrange("p a f -> p (a f)"), ident[:, :])
                    mm.then_inc(xT_done, 1)
                wait(pe, typ_out, g.n)
                for j in range(TG):
                    mm = pe.matmul(typ_ps[:, j * P:(j + 1) * P],
                                   type_b[:, bass.ds(g.n * TG + j, 1)].to_broadcast([P, P]), identb[:, :],
                                   start=True, stop=True)
                mm.then_inc(typ_done, 1)

            def dense_turn(d):
                pe.wait_ge(x_loaded[d.slot], (d.turn + 1) * DMA + dense_dmas(d))
                wait(pe, dT_out, d.n)
                for j in range(DR // 2):
                    mm = pe.transpose(dT_ps[:, j * P:(j + 1) * P], x_in[:, d.slot, j * P:(j + 1) * P], ident[:, :])
                mm.then_inc(dT_done, 1)

            def dense_y(d):
                pe.wait_ge(dT_out, d.n + 1)
                wait(pe, z_done, d.n)
                for j in range(DR // 2):
                    for n, w in enumerate([bd_res, bd_mix]):
                        mm = pe.matmul(y_ps[:, n, j * P:(j + 1) * P], dT[:, d.slot % 2, j * P:(j + 1) * P], w[:, :],
                                       start=True, stop=True)
                mm.then_inc(y_done, 1)

            def pair(m, k):
                pe.wait_ge(masked, m.n * NK + k + 1)
                b = (m.slot * NK + k) % XM
                for side in range(2):
                    mm = pe.matmul(th_ps[side * D:(side + 1) * D, :], w_pair[:, k, :], xm[:, b, side, :],
                                   start=(k == 0 and side == 0), stop=(k == NK - 1), skip_group_check=True)
                mm.then_inc(pair_done, 1)

            def add_edges(m):
                pe.wait_ge(e_staged[m.slot], (m.turn + 1) * DMA)
                for j in range(TG):
                    mm = pe.matmul(th_ps[D:P, j * P:(j + 1) * P], e_r[:, m.slot, j, :], ident[:, :],
                                   start=(j == 0), stop=False, skip_group_check=True)
                mm.then_inc(edges_in, 1)

            def scores(a):
                pe.wait_ge(prod_done, a.n + 1)
                wait(pe, delta_done, a.n - 1)
                for j in range(TG):
                    mm = pe.matmul(att_ps[:, (a.slot % 2) * TG + j:(a.slot % 2) * TG + j + 1],
                                   prod[:, a.slot % 2, j * P:(j + 1) * P], ones[0:D, :], start=True, stop=True)
                mm.then_inc(att_done, 1)

            def step(g):
                if live(g, 1):
                    wait(pe, prod_done, g.n - 1)
                    add_edges(g.back(1))
                    pair(g.back(1), 0)
                if live(g, 2):
                    scores(g.back(2))
                if live(g, 1):
                    dense_y(g.back(1))
                    pair(g.back(1), 1)
                if live(g):
                    turn_in(g)
                    dense_turn(g)
                if live(g, 1):
                    for k in range(2, NK):
                        pair(g.back(1), k)
            run_groups(pe, step, NG, 2)

            pe.wait_ge(max_done, NG)
            pe.matmul(typ_ps[:, 0:P], m_all[:, T:T + 1].to_broadcast([P, P]), ident[:, :], start=True, stop=True)
            pe.matmul(typ_ps[:, P:2 * P], dst_f[:, T - 1:T].to_broadcast([P, P]), ident[:, :],
                      start=True, stop=True).then_inc(ex_pe, 1)
            pe.wait_ge(ex_v, 6)
            pe.transpose(typ_ps[:, 2 * P:3 * P], mats[:, 3, :], ident[:, :]).then_inc(ex_pe, 1)
            pe.wait_ge(ex_v, 7)
            pe.wait_ge(sum_step, NG * TG)
            pe.wait_ge(den_done, NG)
            pe.matmul(att_ps[:, P:P + D], mats[:, 4, :], es_all[:, T, :], start=True, stop=True)
            pe.matmul(att_ps[:, P + D:P + D + 1], mats[:, 4, :], s_all[:, T:T + 1], start=True, stop=True).then_inc(ex_pe, 1)

            def final(g):
                b = g.slot % 2
                pe.wait_ge(uw_done, g.n + 1)
                wait(pe, uwT_out, g.n - 1)
                for j in range(TG):
                    mm = pe.transpose(xT_ps[:, b, j * P:(j + 1) * P], xm[:, b, 0, j * P:(j + 1) * P], ident[:, :])
                mm.then_inc(uwT_done, 1)
                pe.wait_ge(uwT_out, g.n + 1)
                wait(pe, z3_done, g.n - 1)
                for j in range(TG):
                    uwT = xm[:, b, 1, j * P:(j + 1) * P]
                    pe.matmul([th_ps, dT_ps][b][:, j * P:(j + 1) * P], uwT, bd_both[:, :], start=True, stop=True)
                    mm = pe.matmul(y_ps[:, b, j * D:(j + 1) * D], uwT, st_mix[:, :], start=True, stop=True)
                mm.then_inc(y3_done, 1)
            run_groups(pe, final, NG, 0)

        @block.scalar
        def _(act):
            act.wait_ge(setup_v, SETUP_V)

            def step(g):
                if live(g):
                    act.wait_ge(gathered[g.slot], (g.turn + 1) * 2 * TG * DMA)
                    act.copy(x_r[:, g.slot, :, :, 1, :], x_r[:, g.slot, :, :, 0, :]).then_inc(twice, 1)
                    act.dma_start(xd_all[:, bass.ds(g.n * TG, TG), :], x_r[:, g.slot, 1, :, 0, :]).then_inc(xd_saved[g.slot], DMA)
                if live(g, 2):
                    squares(g.back(2), DR)
                if live(g, 4):
                    d = g.back(4)
                    normalise(d, DR, z[:, d.slot, :], o[:, d.slot % 2, :])
                    act.wait_ge(norm_done, d.n + 1)
                    dense_dma(act, False, d, o[:, d.slot % 2, :], o_stored[d.slot % 2])
                if live(g, 1):
                    d = g.back(1)
                    act.wait_ge(y_done, d.n + 1)
                    wait(act, z_done, d.n - 1)
                    act.activation(relu[:, d.slot % 2, :], y_ps[:, 0, :], ACT.Relu, scale=1.0 - SLOPE).then_inc(relu_done, 1)
                if live(g):
                    wait(act, masked, (g.n - 1) * NK)
                    for side in range(2):
                        act.wait_ge(xT_done, 2 * g.n + side + 1)
                        act.copy(xT[:, g.slot % 2, side, :], xT_ps[:, side, :]).then_inc(xT_out, 1)
                    act.wait_ge(typ_done, g.n + 1)
                    act.copy(typ[:, g.slot % 2, :], typ_ps[:, :]).then_inc(typ_out, 1)
                    act.wait_ge(dT_done, g.n + 1)
                    wait(act, y_done, g.n - 1)
                    act.copy(dT[:, g.slot % 2, :], dT_ps[:, :]).then_inc(dT_out, 1)
                if live(g, 2):
                    a = g.back(2)
                    b = a.slot % 2
                    wait(act, den_done, a.n - 1)
                    wait(act, sum_step, (a.n - 1) * TG)
                    act.wait_ge(delta_done, a.n + 1)
                    act.activation(wd[:, b, :, :], delta[:, b, :, :], ACT.Exp).then_inc(exp_done, 1)
                    act.wait_ge(exp_done, a.n + 1)
                    for j in range(TG):
                        ins = act.activation(wx[:, b, j, :], x_r[:, a.slot, 0, j, 0, :], ACT.Copy, scale=wd[:, b, 0, j:j + 1])
                    ins.then_inc(wx_done, 1)
                if live(g, 1):
                    m = g.back(1)
                    act.wait_ge(pair_done, (m.n + 1) * NK)
                    wait(act, prod_done, m.n - 1)
                    act.activation(g_r[:, m.slot % 2, :], th_ps[D:P, :], ACT.Tanh).then_inc(tanh_done, 1)

            def squares(d, rows):
                act.wait_ge(mean_done, d.n + 1)
                wait(act, ssq_done, d.n - 1)
                for j in range(rows):
                    ins = act.activation(junk[:, d.slot % 2, j * D:(j + 1) * D], z[:, d.slot, j * D:(j + 1) * D], ACT.Square,
                                         bias=nmean[:, d.slot, j:j + 1], accum_out=ssq[:, d.slot, j:j + 1])
                ins.then_inc(ssq_done, 1)

            def normalise(d, rows, zin, to):
                act.wait_ge(bias_done, d.n + 1)
                n = d.back(2)
                if not known(n.turn) or n.turn >= 0:
                    act.wait_ge(o_stored[d.slot % 2], (n.turn * 2 + n.slot // 2 + 1) * DMA)
                for j in range(rows):
                    ins = act.activation(to[:, j * D:(j + 1) * D], zin[:, j * D:(j + 1) * D], ACT.Identity,
                                         scale=rstd[:, d.slot, j:j + 1], bias=nbias[:, d.slot, j:j + 1])
                ins.then_inc(norm_done, 1)
            run_groups(act, step, NG, 4)
            for q in range(2):
                act.wait_ge(o_stored[q], (-(-(NG - q) // 2)) * DMA + (dense_dmas(Group(NG // RING, 0)) if q == (NG - 1) % 2 else 0))
            act.wait_ge(norm_done, NG)
            act.activation(prev[:, 7:8], nbias[:, 0, 0:1], ACT.Copy).then_inc(dense_stored, 1)
            act.wait_ge(ex_v, 5)
            act.activation(mats[:, 2, :], mats[:, 1, :], ACT.Exp, bias=prev[:, 1:2]).then_inc(ex_act, 1)
            act.wait_ge(ex_v, 13)
            act.activation(tab[:, 5 * T:7 * T], tab[:, 3 * T:5 * T], ACT.Exp).then_inc(ex_act, 1)

            def final(g):
                b = g.slot % 2
                if live(g):
                    act.wait_ge(uwT_done, g.n + 1)
                    wait(act, y3_done, g.n - 1)
                    act.copy(xm[:, b, 1, :], xT_ps[:, b, :]).then_inc(uwT_out, 1)
                if live(g, 1):
                    d = g.back(1)
                    act.wait_ge(mean3_done, d.n + 1)
                    wait(act, sq3_done, d.n - 1)
                    for j in range(TG):
                        ins = act.activation(junk[:, d.slot % 2, j * D:(j + 1) * D], z[:, d.slot, j * D:(j + 1) * D], ACT.Square,
                                             bias=nmean[:, d.slot, j:j + 1], accum_out=ssq[:, d.slot, j:j + 1])
                    ins.then_inc(sq3_done, 1)
                if live(g, 2):
                    d = g.back(2)
                    act.wait_ge(var3_done, d.n + 1)
                    act.activation(rstd[:, d.slot, 0:TG], var[:, d.slot, 0:TG], ACT.Sqrt).then_inc(sqrt3_done, 1)
                if live(g, 3):
                    d = g.back(3)
                    act.wait_ge(bias3_done, d.n + 1)
                    wait(act, scattered[d.slot], d.turn * TG * DMA)
                    for j in range(TG):
                        ins = act.activation(out_r[:, d.slot, j, :], z[:, d.slot, j * D:(j + 1) * D], ACT.Identity,
                                             scale=var[:, d.slot, j:j + 1], bias=nbias[:, d.slot, j:j + 1])
                    ins.then_inc(norm3_done, 1)
                if live(g):
                    act.wait_ge(y3_done, g.n + 1)
                    wait(act, z3_done, g.n - 1)
                    act.activation(relu[:, b, :], [th_ps, dT_ps][b][:, :], ACT.Relu, scale=1.0 - SLOPE).then_inc(relu3_done, 1)
            run_groups(act, final, NG, 3)

        @block.vector
        def _(v):
            v.memset(ends_i[96:P, :, LASTC:T], 0).then_inc(tables_zero, 1)
            v.memset(type_i[96:P, LASTC:T], 0).then_inc(tables_zero, 1)
            v.memset(next_i[:, :], FAR).then_inc(tables_zero, 1)
            v.memset(es_all[96:P, LASTC + 1:T + 1, :], 0.0).then_inc(e_zero, 1)
            v.wait_ge(tables_in, 11 * DMA)
            v.tensor_copy(dst_f0[:, 0:T], ends_i[:, 1, :]).then_inc(setup_v, 1)
            v.tensor_copy(dst_f0[:, T:T + 1], next_i[:, 0:1]).then_inc(setup_v, 1)
            v.tensor_copy(type_b[:, :], type_i[:, :]).then_inc(setup_v, 1)
            v.memset(m_all[:, 0:1], 0.0).then_inc(setup_v, 1)
            v.memset(s_all[:, 0:1], 0.0).then_inc(setup_v, 1)
            v.memset(es_all[:, 0, :], 0.0).then_inc(setup_v, 1)
            v.memset(bd_res[:, :], 0.0).then_inc(setup_v, 1)
            v.memset(bd_both[:, :], 0.0).then_inc(setup_v, 1)
            v.wait_ge(consts, 7)
            v.tensor_copy(identb[:, :], ident[:, :]).then_inc(setup_v, 1)
            v.tensor_copy(relk[0:D, :], relk0[0:D, :]).then_inc(setup_v, 1)
            v.tensor_scalar(relk[D:P, :], relk0[D:P, :], 1.0, None, ALU.add).then_inc(setup_v, 1)
            v.wait_ge(resT, 1)
            v.wait_ge(setup_v, 8)
            for h in range(2):
                q = slice(h * D, (h + 1) * D)
                v.tensor_copy(bd_res[q, q], att_ps[q, 0:D]).then_inc(setup_v, 1)
                v.tensor_copy(bd_both[q, q], att_ps[q, D:2 * D]).then_inc(setup_v, 1)
            v.tensor_scalar(st_mix[:, :], att_ps[:, D:2 * D], SLOPE, None, ALU.mult).then_inc(setup_v, 1)
            v.wait_ge(setup_v, 15)
            v.scalar_tensor_tensor(bd_mix[:, :], bd_res[:, :], SLOPE, ident[:, :], ALU.mult, ALU.add).then_inc(setup_v, 1)
            v.wait_ge(dst_masked, 1)
            v.tensor_tensor(same[:, :], dst_f[:, 0:T], dst_f[:, 1:T + 1], ALU.is_equal).then_inc(setup_v, 1)
            v.tensor_scalar(inf_f[:, :], dst_f[:, 0:T], dst_f[:, 0:1], None, ALU.is_equal).then_inc(setup_v, 1)
            v.wait_ge(setup_v, 18)
            v.memset(start[:, 0:1], -BIG).then_inc(setup_v, 1)
            v.tensor_scalar(start[:, 1:T], same[:, 0:T - 1], -1.0, BIG, ALU.add, ALU.mult).then_inc(setup_v, 1)
            v.scalar_tensor_tensor(row_i[:, :], same[:, :], float(FAR), dst_f[:, 0:T], ALU.mult, ALU.add).then_inc(setup_v, 1)
            v.wait_ge(setup_v, SETUP_V)

            def mask(m, k):
                if k == 0:
                    v.wait_ge(xT_out, 2 * m.n + 2)
                    v.wait_ge(typ_out, m.n + 1)
                wait(v, pair_done, m.n * NK + k + 1 - XM)
                b = (m.slot * NK + k) % XM
                v.scalar_tensor_tensor(xm[:, b, :, :], typ[:, m.slot % 2, :].unsqueeze(1).to_broadcast([P, 2, W]),
                                       relk[:, k:k + 1], xT[:, m.slot % 2, :, :], ALU.is_equal, ALU.mult).then_inc(masked, 1)

            def guess(d, n):
                bits = newt[:, 0, :].bitcast(I32)
                wait(v, newt_step, d.n * 11 + n)
                if n == 0:
                    v.wait_ge(var_done, d.n + 1)
                    v.tensor_scalar(bits, var[:, d.slot, :].bitcast(I32), 1, None, ALU.logical_shift_right).then_inc(newt_step, 1)
                else:
                    v.tensor_scalar(rstd[:, d.slot, :].bitcast(I32), bits, -1.0, float(MAGIC), ALU.mult, ALU.add).then_inc(newt_step, 1)

            def sum_one(s, j):
                v.wait_ge(wx_done, s.n + 1)
                wait(v, sum_step, s.n * TG + j)
                c = s.n * TG + j
                v.scalar_tensor_tensor(es_all[:, bass.ds(c + 1, 1), :].rearrange("p a f -> p (a f)"),
                                       es_all[:, bass.ds(c, 1), :].rearrange("p a f -> p (a f)"),
                                       wd[:, s.slot % 2, 1, j:j + 1], wx[:, s.slot % 2, j, :],
                                       ALU.mult, ALU.add).then_inc(sum_step, 1)

            def refine(d, n):
                y, v_, a, b = rstd[:, d.slot, :], var[:, d.slot, :], newt[:, 0, :], newt[:, 1, :]
                v.wait_ge(newt_step, d.n * 11 + 2 + n)
                if n % 3 == 0:
                    v.tensor_tensor(a, y, y, ALU.mult).then_inc(newt_step, 1)
                elif n % 3 == 1:
                    v.scalar_tensor_tensor(b, a, -0.5, v_, ALU.mult, ALU.mult).then_inc(newt_step, 1)
                else:
                    v.scalar_tensor_tensor(y, b, 1.5, y, ALU.add, ALU.mult).then_inc(newt_step, 1)

            def score_max(a):
                v.wait_ge(att_done, a.n + 1)
                wait(v, max_done, a.n)
                v.tensor_tensor_scan(m_all[:, bass.ds(a.n * TG + 1, TG)], start[:, bass.ds(a.n * TG, TG)],
                                     att_ps[:, (a.slot % 2) * TG:(a.slot % 2) * TG + TG],
                                     m_all[:, bass.ds(a.n * TG, 1)], ALU.add, ALU.max).then_inc(max_done, 1)

            def step(g):
                m, a, s, d, dv, dn = g.back(1), g.back(2), g.back(3), g.back(1), g.back(2), g.back(3)
                main, late, last = live(g, 1), live(g, 2), live(g, 3)
                if main:
                    mask(m, 0)
                if last:
                    guess(dn, 0)
                    sum_one(s, 0)
                    guess(dn, 1)
                if late:
                    v.wait_ge(tanh_done, a.n + 1)
                    wait(v, att_done, a.n - 1)
                    v.tensor_tensor(prod[:, a.slot % 2, :], th_ps[0:D, :], g_r[:, a.slot % 2, :],
                                    ALU.mult).then_inc(prod_done, 1)
                if last:
                    refine(dn, 0)
                if main:
                    mask(m, 1)
                if last:
                    refine(dn, 1)
                    sum_one(s, 1)
                    refine(dn, 2)
                if main:
                    mask(m, 2)
                if last:
                    refine(dn, 3)
                if late:
                    score_max(a)
                if last:
                    sum_one(s, 2)
                    refine(dn, 4)
                if main:
                    mask(m, 3)
                if last:
                    refine(dn, 5)
                if late:
                    b = a.slot % 2
                    col = bass.ds(a.n * TG + 1, TG)
                    v.wait_ge(max_done, a.n + 1)
                    wait(v, exp_done, a.n - 1)
                    v.tensor_tensor(delta[:, b, 1, :], m_all[:, bass.ds(a.n * TG, TG)], m_all[:, col],
                                    ALU.subtract).then_inc(sub_done, 1)
                    v.tensor_tensor(delta[:, b, 0, :], att_ps[:, (a.slot % 2) * TG:(a.slot % 2) * TG + TG],
                                    m_all[:, col], ALU.subtract)
                if last:
                    sum_one(s, 3)
                    refine(dn, 6)
                if late:
                    v.wait_ge(sub_done, a.n + 1)
                    v.tensor_tensor(delta[:, b, 1, :], delta[:, b, 1, :], start[:, bass.ds(a.n * TG, TG)],
                                    ALU.add).then_inc(delta_done, 1)
                if main:
                    mask(m, 4)
                if last:
                    refine(dn, 7)
                if main:
                    wait(v, norm_done, d.n - RING + 1)
                    v.wait_ge(relu_done, d.n + 1)
                    v.tensor_tensor(z[:, d.slot, :], relu[:, d.slot % 2, :], y_ps[:, 1, :], ALU.add).then_inc(z_done, 1)
                if last:
                    refine(dn, 8)
                if late:
                    v.wait_ge(ssq_done, dv.n + 1)
                    v.tensor_scalar(var[:, dv.slot, :], ssq[:, dv.slot, :], 1.0 / D, EPS, ALU.mult, ALU.add).then_inc(var_done, 1)
                if main:
                    v.wait_ge(z_done, d.n + 1)
                    v.tensor_reduce(zsum[:, d.slot, :], z[:, d.slot, :].rearrange("p (j f) -> p j f", f=D), AX.X,
                                    ALU.add).then_inc(zsum_done, 1)
                if last:
                    v.wait_ge(newt_step, dn.n * 11 + 11)
                    v.tensor_tensor(nbias[:, dn.slot, :], nmean[:, dn.slot, :], rstd[:, dn.slot, :], ALU.mult).then_inc(bias_done, 1)
                    b = s.slot % 2
                    wait(v, den_done, s.n)
                    v.tensor_tensor_scan(s_all[:, bass.ds(s.n * TG + 1, TG)], wd[:, b, 1, :], wd[:, b, 0, :],
                                         s_all[:, bass.ds(s.n * TG, 1)], ALU.mult, ALU.add).then_inc(den_done, 1)
                if main:
                    v.wait_ge(zsum_done, d.n + 1)
                    v.tensor_scalar(nmean[:, d.slot, :], zsum[:, d.slot, :], -1.0 / D, None, ALU.mult).then_inc(mean_done, 1)
            run_groups(v, step, NG, 3)

            msk, aa = mats[:, 0, :], mats[:, 1, :]
            v.wait_ge(ex_pe, 1)
            v.scalar_tensor_tensor(msk, typ_ps[:, P:2 * P], dst_f[:, 0:1], before[:, :], ALU.is_equal, ALU.mult).then_inc(ex_v, 1)
            v.wait_ge(ex_v, 1)
            v.tensor_tensor(aa, typ_ps[:, 0:P], msk, ALU.mult).then_inc(ex_v, 1)
            v.tensor_scalar(mats[:, 2, :], msk, -1.0, NONE, ALU.add, ALU.mult).then_inc(ex_w, 1)
            v.wait_ge(ex_v, 2)
            v.wait_ge(ex_w, 1)
            v.tensor_tensor(aa, aa, mats[:, 2, :], ALU.add).then_inc(ex_v, 1)
            v.wait_ge(ex_v, 3)
            v.tensor_reduce(prev[:, 0:1], aa, AX.X, ALU.max).then_inc(ex_v, 1)
            v.wait_ge(ex_v, 4)
            v.tensor_scalar(prev[:, 1:2], prev[:, 0:1], -1.0, None, ALU.mult).then_inc(ex_v, 1)
            v.wait_ge(ex_act, 1)
            v.tensor_tensor(mats[:, 3, :], mats[:, 2, :], msk, ALU.mult).then_inc(ex_v, 1)
            v.wait_ge(ex_pe, 2)
            v.tensor_copy(mats[:, 4, :], typ_ps[:, 2 * P:3 * P]).then_inc(ex_v, 1)
            t2, mm, da, db, ea, eb = (tab[:, k * T:(k + 1) * T] for k in (2, 7, 3, 4, 5, 6))
            own, den = tab[:, 8 * T:9 * T], tab[:, 9 * T:10 * T]
            v.wait_ge(z_done, NG)
            v.tensor_scalar(t2, inf_f[:, :], -1.0, NONE, ALU.add, ALU.mult).then_inc(ex_v, 1)
            v.wait_ge(ex_v, 8)
            v.scalar_tensor_tensor(own, inf_f[:, :], prev[:, 0:1], t2, ALU.mult, ALU.add).then_inc(ex_v, 1)
            v.wait_ge(ex_v, 9)
            v.tensor_tensor(mm, m_all[:, 1:T + 1], own, ALU.max).then_inc(ex_v, 1)
            v.wait_ge(ex_v, 10)
            v.tensor_tensor(da, m_all[:, 1:T + 1], mm, ALU.subtract).then_inc(ex_v, 1)
            v.tensor_tensor(db, own, mm, ALU.subtract).then_inc(ex_v, 1)
            v.wait_ge(ex_pe, 3)
            v.tensor_copy(carry[:, :], att_ps[:, P:P + D + 1]).then_inc(ex_v, 1)
            v.wait_ge(ex_v, 13)
            v.wait_ge(ex_act, 2)
            v.tensor_tensor(own, ea, s_all[:, 1:T + 1], ALU.mult).then_inc(ex_v, 1)
            v.wait_ge(ex_v, 14)
            v.scalar_tensor_tensor(den, eb, carry[:, D:D + 1], own, ALU.mult, ALU.add).then_inc(ex_v, 1)
            v.wait_ge(ex_v, 15)
            v.reciprocal(mm, den).then_inc(ex_v, 1)
            v.wait_ge(ex_v, 16)
            v.tensor_tensor(fa, ea, mm, ALU.mult).then_inc(ex_v, 1)
            v.tensor_tensor(fb, eb, mm, ALU.mult).then_inc(ex_v, 1)
            v.wait_ge(ex_v, 18)

            def final(g):
                new, mid, var_, end = live(g), live(g, 1), live(g, 2), live(g, 3)
                b, d1, d2, d3 = g.slot % 2, g.back(1), g.back(2), g.back(3)
                c = d1.slot % 2
                cols = bass.ds(g.n * TG, TG)
                own_, car, h = (xT[:, b, k // 2, (k % 2) * 256:(k % 2) * 256 + 256].rearrange("p (j f) -> p j f", f=D)
                                for k in range(3))
                uw = xm[:, b, 0, :].rearrange("p (j k f) -> p j k f", k=2, f=D)
                r2 = relu[:, c, :].rearrange("p (j k f) -> p j k f", k=2, f=D)
                za, zb = (prod_ex[:, c, k, :] for k in range(2))
                if new:
                    wait(v, h_step, (g.n - 1) * 3)
                    v.tensor_tensor(own_, es_all[:, bass.ds(g.n * TG + 1, TG), :],
                                    fa[:, cols].unsqueeze(2).to_broadcast([P, TG, D]), ALU.mult).then_inc(h_step, 1)
                    v.tensor_tensor(car, carry[:, 0:D].unsqueeze(1).to_broadcast([P, TG, D]),
                                    fb[:, cols].unsqueeze(2).to_broadcast([P, TG, D]), ALU.mult).then_inc(h_step, 1)
                if var_:
                    v.wait_ge(sq3_done, d2.n + 1)
                    v.tensor_scalar(var[:, d2.slot, 0:TG], ssq[:, d2.slot, 0:TG], 1.0 / D, EPS, ALU.mult, ALU.add).then_inc(var3_done, 1)
                if end:
                    wait(v, scattered[d3.slot], d3.turn * TG * DMA)
                    v.tensor_copy(row_r[:, d3.slot, :], row_i[:, bass.ds(d3.n * TG, TG)]).then_inc(row_done, 1)
                    v.wait_ge(sqrt3_done, d3.n + 1)
                    v.reciprocal(var[:, d3.slot, 0:TG], rstd[:, d3.slot, 0:TG]).then_inc(rec3_done, 1)
                if new:
                    v.wait_ge(h_step, g.n * 3 + 2)
                    v.tensor_tensor(h, own_, car, ALU.add).then_inc(h_step, 1)
                if end:
                    v.wait_ge(rec3_done, d3.n + 1)
                    v.tensor_tensor(nbias[:, d3.slot, 0:TG], nmean[:, d3.slot, 0:TG], var[:, d3.slot, 0:TG],
                                    ALU.mult).then_inc(bias3_done, 1)
                if mid:
                    v.wait_ge(relu3_done, d1.n + 1)
                    wait(v, z3_done, d1.n - 1)
                    v.tensor_tensor(za.rearrange("p (j f) -> p j f", f=D), r2[:, :, 0, :], r2[:, :, 1, :], ALU.add).then_inc(za_done, 1)
                    v.tensor_tensor(zb.rearrange("p (j f) -> p j f", f=D),
                                    y_ps[:, c, 0:TG * D].rearrange("p (j f) -> p j f", f=D),
                                    xd_all[:, bass.ds(d1.n * TG, TG), :], ALU.add).then_inc(za_done, 1)
                if new:
                    v.wait_ge(h_step, g.n * 3 + 3)
                    wait(v, uwT_done, g.n - 1)
                    xd = xd_all[:, cols, :]
                    v.tensor_tensor(uw[:, :, 0, :], h, xd, ALU.add)
                if mid:
                    v.wait_ge(za_done, 2 * d1.n + 2)
                    wait(v, norm3_done, d1.n - RING + 1)
                    v.tensor_tensor(z[:, d1.slot, 0:TG * D], za, zb, ALU.add).then_inc(z3_done, 1)
                if new:
                    v.tensor_tensor(uw[:, :, 1, :], h, xd, ALU.mult).then_inc(uw_done, 1)
                if mid:
                    v.wait_ge(z3_done, d1.n + 1)
                    v.tensor_reduce(zsum[:, d1.slot, 0:TG], z[:, d1.slot, 0:TG * D].rearrange("p (j f) -> p j f", f=D), AX.X,
                                    ALU.add).then_inc(zsum3_done, 1)
                    v.wait_ge(zsum3_done, d1.n + 1)
                    v.tensor_scalar(nmean[:, d1.slot, 0:TG], zsum[:, d1.slot, 0:TG], -1.0 / D, None, ALU.mult).then_inc(mean3_done, 1)
            run_groups(v, final, NG, 3)


def kernel(**inputs):
    import numpy as np
    import concourse.bacc as bacc
    from concourse.bass_utils import run_bass_kernel_spmd

    nc = bacc.Bacc("TRN2", target_bir_lowering=False, num_devices=1)
    arrays, args = {}, []
    for name in ["x", "src", "dst", "edge_attr_64", "edge_type_10", "L0_gnn_relation_weight", "L0_gnn_res_fc_w",
                 "L0_gnn_res_fc2_w"]:
        a = np.ascontiguousarray(inputs[name])
        arrays[f"in_{name}"] = a
        args.append(nc.dram_tensor(f"in_{name}", a.shape, mybir.dt.from_np(a.dtype), kind="ExternalInput").ap())
    args.append(nc.dram_tensor("out", inputs["x"].shape, F32, kind="ExternalOutput").ap())
    gnn_resnorm(nc, *args)
    return run_bass_kernel_spmd(nc, [arrays], core_ids=[0]).results[0]["out"]
```

```python
from contextlib import ExitStack

import concourse.bass as bass
from concourse import mybir

ALU = mybir.AluOpType
ACT = mybir.ActivationFunctionType
AX = mybir.AxisListType
F32 = mybir.dt.float32
BF16 = mybir.dt.bfloat16
I32 = mybir.dt.int32

P = 128
DMA = 16
TG = 4
TURNS = 2
RING = 4
BIG = 3.0e38
NONE = 1.0e30
FAR = 1 << 20
SLOPE = 0.01
EPS = 1e-5
MAGIC = 0x5F3759DF
XM = 4


class Group:

    def __init__(self, turn, slot):
        self.turn, self.slot = turn, slot
        self.n = turn * RING + slot

    def back(self, k):
        turn, slot = self.turn, self.slot - k
        while slot < 0:
            turn, slot = turn - 1, slot + RING
        return Group(turn, slot)


def known(v):
    return isinstance(v, int)


def wait(eng, sem, value):
    if not known(value) or value > 0:
        eng.wait_ge(sem, value)


def hold(pool, tile, done, g):
    wait(pool, done, g.n - RING + 1)
    pool.tensor_tensor(tile[:, g.slot + 1:g.slot + 2], tile[:, 0:1], tile[:, 0:1], ALU.add).then_inc(done, 1)


def run_groups(eng, step, groups, lag, first=None):
    if first is None:
        first = 1 if lag == 0 else 2 if lag < 5 else 3
    rounds = (groups // RING - first) // TURNS
    last = first + rounds * TURNS
    for it in range(first * RING):
        step(Group(it // RING, it % RING))
    with eng.Fori(0, rounds) as r:
        for k in range(TURNS):
            for slot in range(RING):
                step(Group(r * TURNS + (first + k), slot))
    for it in range(last * RING, groups + lag):
        step(Group(it // RING, it % RING))


def gnn_resnorm(nc, x, src, dst, eattr, etype, relw, resw, resw2, out):
    N, D = x.shape
    E = src.shape[0]
    R = relw.shape[0]
    T = -(-E // P)
    NG = T // TG
    assert T % TG == 0 and D == 64 and R % 2 == 0
    NK = R // 2
    LASTC = E - (P - 1) * T
    W = TG * P
    DR = -(-N // (NG * P))
    DB = P * DR
    DLAST = N - (NG - 1) * DB
    assert DR % 2 == 0 and DR * D == 512 and DLAST % DR == 0 and 0 < LASTC < T
    PL = DLAST // DR
    PL0 = PL // DMA * DMA

    with ExitStack() as ctx:
        def sb(name, shape, dt=F32):
            return ctx.enter_context(nc.sbuf_tensor(name, shape, dt))

        def ps(name, shape):
            return ctx.enter_context(nc.psum_tensor(name, shape, F32))

        def sem(name):
            return ctx.enter_context(nc.semaphore(name))

        ident = sb("ident", [P, P])
        identb = sb("identb", [P, P], BF16)
        ones = sb("ones", [P, 1])
        relk0 = sb("relk0", [P, NK])
        relk = sb("relk", [P, NK])
        before = sb("before", [P, P])
        w_pair = sb("w_pair", [P, NK, D])
        res_rows = sb("res_rows", [D, 3 * D])
        bd_res = sb("bd_res", [P, P])
        bd_mix = sb("bd_mix", [P, P])
        bd_both = sb("bd_both", [P, P])
        st_mix = sb("st_mix", [P, D])
        ends_i = sb("ends_i", [P, 2, T], I32)
        next_i = sb("next_i", [P, 2], I32)
        type_i = sb("type_i", [P, T], I32)
        type_b = sb("type_b", [P, T], BF16)
        dst_f0 = sb("dst_f0", [P, T + 1])
        dst_f = sb("dst_f", [P, T + 1])
        same = sb("same", [P, T])
        start = sb("start", [P, T])
        row_i = sb("row_i", [P, T], I32)
        inf_f = sb("inf_f", [P, T])
        m_all = sb("m_all", [P, T + 1])
        s_all = sb("s_all", [P, T + 1])
        es_all = sb("es_all", [P, T + 1, D])
        xd_all = sb("xd_all", [P, T, D])
        idx = sb("idx", [P, RING, 2, TG], I32)
        x_r = sb("x_r", [P, RING, 2, TG, 2, D])
        e_r = sb("e_r", [P, RING, TG, D])
        xT = sb("xT", [P, 2, 2, W])
        typ = sb("typ", [P, 2, W])
        xm = sb("xm", [P, XM, 2, W])
        g_r = sb("g_r", [D, 2, W])
        prod = sb("prod", [D, 2, W])
        delta = sb("delta", [P, 2, 2, TG])
        wd = sb("wd", [P, 2, 2, TG])
        wx = sb("wx", [P, 2, TG, D])
        x_in = sb("x_in", [P, RING, DR * D])
        dT = sb("dT", [P, 2, 512])
        relu = sb("relu", [P, 2, 512])
        z = sb("z", [P, RING, DR * D])
        o = sb("o", [P, 2, DR * D])
        junk = sb("junk", [P, 2, DR * D])
        held = sb("held", [P, 2, RING + 1])
        newt = sb("newt", [P, 2, DR])
        row_r = sb("row_r", [P, RING, TG], I32)
        out_r = sb("out_r", [P, RING, TG, D])
        prev = sb("prev", [P, 8])
        carry = sb("carry", [P, D + 1])
        zsum = sb("zsum", [P, RING, DR])
        nmean = sb("nmean", [P, RING, DR])
        ssq = sb("ssq", [P, RING, DR])
        var = sb("var", [P, RING, DR])
        rstd = sb("rstd", [P, RING, DR])
        nbias = sb("nbias", [P, RING, DR])

        xT_ps = ps("xT_ps", [P, 2, W])
        typ_ps = ps("typ_ps", [P, W])
        th_ps = ps("th_ps", [P, W])
        att_ps = ps("att_ps", [P, 512])
        dT_ps = ps("dT_ps", [P, 512])
        y_ps = ps("y_ps", [P, 2, 512])

        tab = x_in.rearrange("p a b -> p (a b)")
        mats = e_r.rearrange("p a b f -> p (a b f)")[:, 0:5 * P].rearrange("p (k q) -> p k q", q=P)
        prod_ex = o.rearrange("p a (k f) -> p a k f", k=2)
        fa, fb = tab[:, 0:T], tab[:, T:2 * T]

        tables_zero, ends_in, tables_in, w_in, e_in = sem("tables_zero"), sem("ends_in"), sem("tables_in"), sem("w_in"), [sem(f"e_in{i}") for i in range(5)]
        edges_in, twice, sub_done, e_zero = sem("edges_in"), sem("twice"), sem("sub_done"), sem("e_zero")
        consts, dst_masked = sem("consts"), sem("dst_masked")
        setup_v, resT = sem("setup_v"), sem("resT")
        idx_in = [sem(f"idx_in{i}") for i in range(RING)]
        e_staged = [sem(f"e_staged{i}") for i in range(RING)]
        gathered = [sem(f"gathered{i}") for i in range(RING)]
        xd_saved = [sem(f"xd_saved{i}") for i in range(RING)]
        x_loaded = [sem(f"x_loaded{i}") for i in range(RING)]
        o_stored = [sem(f"o_stored{i}") for i in range(2)]
        xT_done, xT_out, typ_done, typ_out = sem("xT_done"), sem("xT_out"), sem("typ_done"), sem("typ_out")
        masked, pair_done = sem("masked"), sem("pair_done")
        tanh_done, prod_done, att_done, max_done = sem("tanh_done"), sem("prod_done"), sem("att_done"), sem("max_done")
        delta_done, exp_done, wx_done, sum_step, den_done = (
            sem("delta_done"), sem("exp_done"), sem("wx_done"), sem("sum_step"), sem("den_done"))
        dT_done, dT_out, y_done, relu_done, z_done = (
            sem("dT_done"), sem("dT_out"), sem("y_done"), sem("relu_done"), sem("z_done"))
        held_gather, held_scatter = sem("held_gather"), sem("held_scatter")
        newt_step, dense_stored = sem("newt_step"), sem("dense_stored")
        ex_pe, ex_v, ex_w, ex_act = sem("ex_pe"), sem("ex_v"), sem("ex_w"), sem("ex_act")
        scattered = [sem(f"scattered{i}") for i in range(RING)]
        row_done, h_step, uw_done, uwT_done, uwT_out, y3_done, relu3_done, za_done, z3_done, zsum3_done = (
            sem(n) for n in ["row_done", "h_step", "uw_done", "uwT_done", "uwT_out", "y3_done", "relu3_done", "za_done",
                             "z3_done", "zsum3_done"])
        mean3_done, sq3_done, var3_done, sqrt3_done, rec3_done, bias3_done, norm3_done = (
            sem(n) for n in ["mean3_done", "sq3_done", "var3_done", "sqrt3_done", "rec3_done", "bias3_done", "norm3_done"])
        zsum_done, mean_done, ssq_done, var_done, bias_done, norm_done = (
            sem("zsum_done"), sem("mean_done"), sem("ssq_done"), sem("var_done"), sem("bias_done"), sem("norm_done"))

        SETUP_V = 22
        E_PARTS = [0, 4 * TG, 16 * TG, 27 * TG, 38 * TG, T]
        EP = len(E_PARTS) - 1
        E_WAITS = {0: [0], RING: [1], 2 * RING - 1: range(2, EP)}

        OUT_LAG = 7

        def live(g, k=0):
            return not known(g.turn) or 0 <= g.n - k < NG

        def dense_dma(eng, to_sbuf, d, tile, done):
            dram = x if to_sbuf else out
            if known(d.turn) and d.n == NG - 1:
                parts = [(0, PL0), (PL0, PL)] if PL0 < PL else [(0, PL)]
            else:
                parts = [(0, P)]
            for a, b in parts:
                rows = dram[bass.ds(d.n * DB + a * DR, (b - a) * DR), :].rearrange("(p j) f -> p (j f)", j=DR)
                if to_sbuf:
                    eng.dma_start(tile[a:b, :], rows).then_inc(done, DMA)
                else:
                    eng.dma_start(rows, tile[a:b, :]).then_inc(done, DMA)

        def dense_dmas(d):
            return DMA if known(d.turn) and d.n == NG - 1 and PL0 < PL else 0

        block = ctx.enter_context(nc.Block())

        @block.sync
        def _(sp):
            def table(dram, tile, done):
                rows = dram[0:(P - 1) * T].rearrange("(p c) -> p c", c=T)
                a = (P - 1) // DMA * DMA
                sp.dma_start(tile[0:a, 0:T], rows[0:a, :]).then_inc(done, DMA)
                sp.dma_start(tile[a:P - 1, 0:T], rows[a:P - 1, :]).then_inc(done, DMA)
                sp.dma_start(tile[P - 1:P, 0:LASTC], dram[(P - 1) * T:E].rearrange("(a c) -> a c", a=1)).then_inc(done, DMA)
            sp.wait_ge(tables_zero, 3)
            table(src, ends_i[:, 0, :], ends_in)
            table(dst, ends_i[:, 1, :], ends_in)
            table(etype, type_i[:, :], tables_in)
            heads = dst[T:(P - 1) * T].rearrange("(p c) -> p c", c=T)
            sp.dma_start(next_i[0:P - 2, :], heads[:, 0:2]).then_inc(tables_in, DMA)
            sp.dma_start(next_i[P - 2:P - 1, :], dst[(P - 1) * T:(P - 1) * T + 2].rearrange("(a c) -> a c", a=1)).then_inc(tables_in, DMA)
            for h in range(2):
                sp.dma_start(w_pair[h * D:(h + 1) * D, :, :],
                             relw.rearrange("(k h) i o -> h i k o", h=2)[h]).then_inc(w_in, DMA)
            for n, w in enumerate([resw, resw, resw2]):
                sp.dma_start(res_rows[:, n * D:(n + 1) * D], w[:, :]).then_inc(w_in, DMA)
            rows = eattr[0:(P - 1) * T, :].rearrange("(p c) f -> p c f", c=T)
            a = (P - 1) // DMA * DMA
            last = eattr[(P - 1) * T:E, :].rearrange("(a c) f -> a c f", a=1)

            def load_edges(n):
                c0, c1 = E_PARTS[n], E_PARTS[n + 1]
                c2 = min(c1, LASTC)
                done = e_in[n]
                sp.dma_start(es_all[0:a, c0 + 1:c1 + 1, :], rows[0:a, c0:c1, :]).then_inc(done, DMA)
                sp.dma_start(es_all[a:P - 1, c0 + 1:c1 + 1, :], rows[a:P - 1, c0:c1, :]).then_inc(done, DMA)
                if c0 < c2:
                    sp.dma_start(es_all[P - 1:P, c0 + 1:c2 + 1, :], last[:, c0:c2, :]).then_inc(done, DMA)
            sp.wait_ge(ends_in, 6 * DMA)

            def step(g):
                if live(g, RING):
                    d = g.back(RING)
                    sp.wait_ge(gathered[d.slot], (d.turn + 1) * 2 * TG * DMA)
                    sp.dma_start(xd_all[:, bass.ds(d.n * TG, TG), :], x_r[:, d.slot, 1, :, 0, :]).then_inc(xd_saved[d.slot], DMA)
                if live(g):
                    sp.dma_start(idx[:, g.slot, :, :], ends_i[:, :, bass.ds(g.n * TG, TG)]).then_inc(idx_in[g.slot], DMA)
                    wait(sp, z_done, g.n - RING + 1)
                    dense_dma(sp, True, g, x_in[:, g.slot, :], x_loaded[g.slot])
                    if known(g.turn) and g.n == 0:
                        sp.wait_ge(e_zero, 1)
                        load_edges(0)
                    if known(g.turn) and RING <= g.n < RING + EP - 1:
                        load_edges(g.n - RING + 1)
                    if known(g.turn) and g.n in E_WAITS:
                        for n in E_WAITS[g.n]:
                            sp.wait_ge(e_in[n], (2 + (E_PARTS[n] < LASTC)) * DMA)
                    wait(sp, edges_in, g.n - RING + 1)
                    sp.dma_start(e_r[:, g.slot, :, :], es_all[:, bass.ds(g.n * TG + 1, TG), :]).then_inc(e_staged[g.slot], DMA)
                if live(g, OUT_LAG):
                    d = g.back(OUT_LAG)
                    sp.wait_ge(norm_done, d.n + 1)
                    dense_dma(sp, False, d, o[:, d.slot % 2, :], o_stored[d.slot % 2])
            run_groups(sp, step, NG, OUT_LAG, first=2)

        @block.gpsimd
        def _(pool):
            pool.memset(ones[:, :], 1.0).then_inc(consts, 1)
            pool.memset(held[:, :, 0:1], 0.0).then_inc(consts, 1)
            pool.memset(ident[:, :], 0.0).then_inc(consts, 1)
            pool.memset(before[:, :], 1.0).then_inc(consts, 1)
            pool.iota(relk0[:, :], [[2, NK]], base=0, channel_multiplier=0,
                      allow_small_or_imprecise_dtypes=True).then_inc(consts, 1)
            pool.wait_ge(consts, 5)
            pool.affine_select(ident[:, :], ident[:, :], [[-1, P]], ALU.not_equal, 1.0, base=0,
                               channel_multiplier=1).then_inc(consts, 1)
            pool.affine_select(before[:, :], before[:, :], [[-1, P]], ALU.is_ge, 0.0, base=-1,
                               channel_multiplier=1).then_inc(consts, 1)
            pool.wait_ge(setup_v, 2)
            pool.affine_select(dst_f[:, :], dst_f0[:, :], [[-1, T + 1]], ALU.is_ge, float(FAR),
                               base=E - 1, channel_multiplier=-T).then_inc(dst_masked, 1)

            def step(g):
                if live(g):
                    pool.wait_ge(idx_in[g.slot], (g.turn + 1) * DMA)
                    wait(pool, wx_done, g.n - RING + 1)
                    wait(pool, xd_saved[g.slot], g.turn * DMA)
                    hold(pool, held[:, 0, :], held_gather, g)
                if live(g):
                    for j in range(TG):
                        for side in range(2):
                            pool.indirect_dma_start(
                                x_r[:, g.slot, side, j, 0, :], None, x[:, :],
                                bass.IndirectOffsetOnAxis(ap=idx[:, g.slot, side, j:j + 1], axis=0),
                            ).then_inc(gathered[g.slot], DMA)
            run_groups(pool, step, NG, 0)

            def scatter(g):
                pool.wait_ge(row_done, g.n + 1)
                pool.wait_ge(norm3_done, g.n + 1)
                hold(pool, held[:, 1, :], held_scatter, g)
                for j in range(TG):
                    pool.indirect_dma_start(
                        out[:, :], bass.IndirectOffsetOnAxis(ap=row_r[:, g.slot, j:j + 1], axis=0),
                        out_r[:, g.slot, j, :], None, bounds_check=top, oob_is_err=False,
                    ).then_inc(scattered[g.slot], DMA)
            pool.wait_ge(dense_stored, 1)
            top = pool.to_reg(N - 1)
            run_groups(pool, scatter, NG, 0)
            for q in range(RING):
                pool.wait_ge(scattered[q], -(-(NG - q) // RING) * TG * DMA)

        @block.tensor
        def _(pe):
            pe.wait_ge(w_in, 5 * DMA)
            pe.wait_ge(consts, 7)
            pe.transpose(att_ps[:, 0:D], res_rows[:, 0:2 * D], ident[0:D, 0:D])
            pe.transpose(att_ps[:, D:2 * D], res_rows[:, D:3 * D], ident[0:D, 0:D]).then_inc(resT, 1)
            pe.wait_ge(setup_v, SETUP_V)

            def turn_in(g):
                pe.wait_ge(twice, g.n + 1)
                wait(pe, xT_out, 2 * g.n)
                for side in range(2):
                    for j in range(TG):
                        mm = pe.transpose(xT_ps[:, side, j * P:(j + 1) * P],
                                          x_r[:, g.slot, side, j, :, :].rearrange("p a f -> p (a f)"), ident[:, :])
                    mm.then_inc(xT_done, 1)
                wait(pe, typ_out, g.n)
                for j in range(TG):
                    mm = pe.matmul(typ_ps[:, j * P:(j + 1) * P],
                                   type_b[:, bass.ds(g.n * TG + j, 1)].to_broadcast([P, P]), identb[:, :],
                                   start=True, stop=True)
                mm.then_inc(typ_done, 1)

            def dense_turn(d):
                pe.wait_ge(x_loaded[d.slot], (d.turn + 1) * DMA + dense_dmas(d))
                wait(pe, dT_out, d.n)
                for j in range(DR // 2):
                    mm = pe.transpose(dT_ps[:, j * P:(j + 1) * P], x_in[:, d.slot, j * P:(j + 1) * P], ident[:, :])
                mm.then_inc(dT_done, 1)

            def dense_y(d):
                pe.wait_ge(dT_out, d.n + 1)
                wait(pe, z_done, d.n)
                for j in range(DR // 2):
                    for n, w in enumerate([bd_res, bd_mix]):
                        mm = pe.matmul(y_ps[:, n, j * P:(j + 1) * P], dT[:, d.slot % 2, j * P:(j + 1) * P], w[:, :],
                                       start=True, stop=True)
                mm.then_inc(y_done, 1)

            def pair(m, k):
                pe.wait_ge(masked, m.n * NK + k + 1)
                b = (m.slot * NK + k) % XM
                for side in range(2):
                    mm = pe.matmul(th_ps[side * D:(side + 1) * D, :], w_pair[:, k, :], xm[:, b, side, :],
                                   start=(k == 0 and side == 0), stop=(k == NK - 1), skip_group_check=True)
                mm.then_inc(pair_done, 1)

            def add_edges(m):
                pe.wait_ge(e_staged[m.slot], (m.turn + 1) * DMA)
                for j in range(TG):
                    mm = pe.matmul(th_ps[D:P, j * P:(j + 1) * P], e_r[:, m.slot, j, :], ident[:, :],
                                   start=(j == 0), stop=False, skip_group_check=True)
                mm.then_inc(edges_in, 1)

            def scores(a):
                pe.wait_ge(prod_done, a.n + 1)
                wait(pe, delta_done, a.n - 1)
                for j in range(TG):
                    mm = pe.matmul(att_ps[:, (a.slot % 2) * TG + j:(a.slot % 2) * TG + j + 1],
                                   prod[:, a.slot % 2, j * P:(j + 1) * P], ones[0:D, :], start=True, stop=True)
                mm.then_inc(att_done, 1)

            def step(g):
                if live(g):
                    turn_in(g)
                if live(g):
                    dense_turn(g)
                if live(g, 1):
                    dense_y(g.back(1))
                if live(g, 2):
                    scores(g.back(2))
                if live(g, 1):
                    wait(pe, prod_done, g.n - 1)
                    add_edges(g.back(1))
                if live(g, 1):
                    pair(g.back(1), 0)
                if live(g, 1):
                    pair(g.back(1), 1)
                if live(g, 1):
                    pair(g.back(1), 2)
                if live(g, 1):
                    pair(g.back(1), 3)
                if live(g, 1):
                    pair(g.back(1), 4)
            run_groups(pe, step, NG, 2)

            pe.wait_ge(max_done, NG)
            pe.matmul(typ_ps[:, 0:P], m_all[:, T:T + 1].to_broadcast([P, P]), ident[:, :], start=True, stop=True)
            pe.matmul(typ_ps[:, P:2 * P], dst_f[:, T - 1:T].to_broadcast([P, P]), ident[:, :],
                      start=True, stop=True).then_inc(ex_pe, 1)
            pe.wait_ge(ex_v, 11)
            pe.transpose(typ_ps[:, 2 * P:3 * P], mats[:, 3, :], ident[:, :]).then_inc(ex_pe, 1)
            pe.wait_ge(ex_v, 12)
            pe.wait_ge(sum_step, NG * TG)
            pe.wait_ge(den_done, NG)
            pe.matmul(att_ps[:, P:P + D], mats[:, 4, :], es_all[:, T, :], start=True, stop=True)
            pe.matmul(att_ps[:, P + D:P + D + 1], mats[:, 4, :], s_all[:, T:T + 1], start=True, stop=True).then_inc(ex_pe, 1)

            def final(g):
                if live(g, 1):
                    d = g.back(1)
                    c = d.slot % 2
                    pe.wait_ge(uwT_out, d.n + 1)
                    wait(pe, z3_done, d.n - 1)
                    for j in range(TG):
                        uwT = xm[:, c, 1, j * P:(j + 1) * P]
                        pe.matmul([th_ps, dT_ps][c][:, j * P:(j + 1) * P], uwT, bd_both[:, :], start=True, stop=True)
                        mm = pe.matmul(y_ps[:, c, j * D:(j + 1) * D], uwT, st_mix[:, :], start=True, stop=True)
                    mm.then_inc(y3_done, 1)
                if live(g):
                    b = g.slot % 2
                    pe.wait_ge(uw_done, g.n + 1)
                    wait(pe, uwT_out, g.n - 1)
                    for j in range(TG):
                        mm = pe.transpose(xT_ps[:, b, j * P:(j + 1) * P], xm[:, b, 0, j * P:(j + 1) * P], ident[:, :])
                    mm.then_inc(uwT_done, 1)
            run_groups(pe, final, NG, 1)

        @block.scalar
        def _(act):
            act.wait_ge(setup_v, SETUP_V)

            def dense_out(g):
                d = g.back(4)
                normalise(d, DR, z[:, d.slot, :], o[:, d.slot % 2, :])

            def exchange():
                act.wait_ge(ex_v, 5)
                act.activation(mats[:, 2, :], mats[:, 1, :], ACT.Exp, bias=prev[:, 1:2]).then_inc(ex_act, 1)
                act.wait_ge(ex_v, 10)
                act.activation(tab[:, 5 * T:7 * T], tab[:, 3 * T:5 * T], ACT.Exp).then_inc(ex_act, 1)

            def step(g):
                ending = known(g.turn) and g.n > NG
                if live(g):
                    act.wait_ge(gathered[g.slot], (g.turn + 1) * 2 * TG * DMA)
                    act.copy(x_r[:, g.slot, :, :, 1, :], x_r[:, g.slot, :, :, 0, :]).then_inc(twice, 1)
                if live(g, 2) and not ending:
                    squares(g.back(2), DR)
                if live(g, 4) and not ending:
                    dense_out(g)
                if live(g, 1):
                    d = g.back(1)
                    act.wait_ge(y_done, d.n + 1)
                    wait(act, z_done, d.n - 1)
                    act.activation(relu[:, d.slot % 2, :], y_ps[:, 0, :], ACT.Relu, scale=1.0 - SLOPE).then_inc(relu_done, 1)
                if live(g):
                    wait(act, masked, (g.n - 1) * NK)
                    for side in range(2):
                        act.wait_ge(xT_done, 2 * g.n + side + 1)
                        act.copy(xT[:, g.slot % 2, side, :], xT_ps[:, side, :]).then_inc(xT_out, 1)
                    act.wait_ge(typ_done, g.n + 1)
                    act.copy(typ[:, g.slot % 2, :], typ_ps[:, :]).then_inc(typ_out, 1)
                    act.wait_ge(dT_done, g.n + 1)
                    wait(act, y_done, g.n - 1)
                    act.copy(dT[:, g.slot % 2, :], dT_ps[:, :]).then_inc(dT_out, 1)
                if live(g, 2):
                    a = g.back(2)
                    b = a.slot % 2
                    wait(act, den_done, a.n - 1)
                    wait(act, sum_step, (a.n - 1) * TG)
                    act.wait_ge(delta_done, a.n + 1)
                    act.activation(wd[:, b, :, :], delta[:, b, :, :], ACT.Exp).then_inc(exp_done, 1)
                    act.wait_ge(exp_done, a.n + 1)
                    for j in range(TG):
                        ins = act.activation(wx[:, b, j, :], x_r[:, a.slot, 0, j, 0, :], ACT.Copy, scale=wd[:, b, 0, j:j + 1])
                    ins.then_inc(wx_done, 1)
                if live(g, 1):
                    m = g.back(1)
                    act.wait_ge(pair_done, (m.n + 1) * NK)
                    wait(act, prod_done, m.n - 1)
                    act.activation(g_r[:, m.slot % 2, :], th_ps[D:P, :], ACT.Tanh).then_inc(tanh_done, 1)
                if ending:
                    if live(g, 2):
                        squares(g.back(2), DR)
                    if g.n == NG + 1:
                        exchange()
                    if live(g, 4):
                        dense_out(g)

            def squares(d, rows):
                act.wait_ge(mean_done, d.n + 1)
                wait(act, ssq_done, d.n - 1)
                for j in range(rows):
                    ins = act.activation(junk[:, d.slot % 2, j * D:(j + 1) * D], z[:, d.slot, j * D:(j + 1) * D], ACT.Square,
                                         bias=nmean[:, d.slot, j:j + 1], accum_out=ssq[:, d.slot, j:j + 1])
                ins.then_inc(ssq_done, 1)

            def normalise(d, rows, zin, to):
                act.wait_ge(bias_done, d.n + 1)
                n = d.back(2)
                if not known(n.turn) or n.turn >= 0:
                    act.wait_ge(o_stored[d.slot % 2], (n.turn * 2 + n.slot // 2 + 1) * DMA)
                for j in range(rows):
                    ins = act.activation(to[:, j * D:(j + 1) * D], zin[:, j * D:(j + 1) * D], ACT.Identity,
                                         scale=rstd[:, d.slot, j:j + 1], bias=nbias[:, d.slot, j:j + 1])
                ins.then_inc(norm_done, 1)
            run_groups(act, step, NG, 4)
            for q in range(2):
                act.wait_ge(o_stored[q], (-(-(NG - q) // 2)) * DMA + (dense_dmas(Group(NG // RING, 0)) if q == (NG - 1) % 2 else 0))
            act.wait_ge(norm_done, NG)
            act.activation(prev[:, 7:8], nbias[:, 0, 0:1], ACT.Copy).then_inc(dense_stored, 1)

            def final(g):
                if live(g, 2):
                    d = g.back(2)
                    c = d.slot % 2
                    act.wait_ge(y3_done, d.n + 1)
                    wait(act, z3_done, d.n - 1)
                    act.activation(relu[:, c, :], [th_ps, dT_ps][c][:, :], ACT.Relu, scale=1.0 - SLOPE).then_inc(relu3_done, 1)
                if live(g, 1):
                    d = g.back(1)
                    c = d.slot % 2
                    act.wait_ge(uwT_done, d.n + 1)
                    wait(act, y3_done, d.n - 1)
                    act.copy(xm[:, c, 1, :], xT_ps[:, c, :]).then_inc(uwT_out, 1)
                if live(g, 4):
                    d = g.back(4)
                    act.wait_ge(var3_done, d.n + 1)
                    act.activation(rstd[:, d.slot, 0:TG], var[:, d.slot, 0:TG], ACT.Sqrt).then_inc(sqrt3_done, 1)
                if live(g, 3):
                    d = g.back(3)
                    act.wait_ge(mean3_done, d.n + 1)
                    wait(act, sq3_done, d.n - 1)
                    for j in range(TG):
                        ins = act.activation(junk[:, d.slot % 2, j * D:(j + 1) * D], z[:, d.slot, j * D:(j + 1) * D], ACT.Square,
                                             bias=nmean[:, d.slot, j:j + 1], accum_out=ssq[:, d.slot, j:j + 1])
                    ins.then_inc(sq3_done, 1)
                if live(g, 5):
                    d = g.back(5)
                    act.wait_ge(bias3_done, d.n + 1)
                    wait(act, scattered[d.slot], d.turn * TG * DMA)
                    for j in range(TG):
                        ins = act.activation(out_r[:, d.slot, j, :], z[:, d.slot, j * D:(j + 1) * D], ACT.Identity,
                                             scale=var[:, d.slot, j:j + 1], bias=nbias[:, d.slot, j:j + 1])
                    ins.then_inc(norm3_done, 1)
            run_groups(act, final, NG, 5)

        @block.vector
        def _(v):
            v.memset(ends_i[96:P, :, LASTC:T], 0).then_inc(tables_zero, 1)
            v.memset(type_i[96:P, LASTC:T], 0).then_inc(tables_zero, 1)
            v.memset(next_i[:, :], FAR).then_inc(tables_zero, 1)
            v.memset(es_all[96:P, LASTC + 1:T + 1, :], 0.0).then_inc(e_zero, 1)
            v.wait_ge(ends_in, 6 * DMA)
            v.wait_ge(tables_in, 5 * DMA)
            v.tensor_copy(dst_f0[:, 0:T], ends_i[:, 1, :]).then_inc(setup_v, 1)
            v.tensor_copy(dst_f0[:, T:T + 1], next_i[:, 0:1]).then_inc(setup_v, 1)
            v.tensor_copy(type_b[:, :], type_i[:, :]).then_inc(setup_v, 1)
            v.memset(m_all[:, 0:1], 0.0).then_inc(setup_v, 1)
            v.memset(s_all[:, 0:1], 0.0).then_inc(setup_v, 1)
            v.memset(es_all[:, 0, :], 0.0).then_inc(setup_v, 1)
            v.memset(bd_res[:, :], 0.0).then_inc(setup_v, 1)
            v.memset(bd_both[:, :], 0.0).then_inc(setup_v, 1)
            v.wait_ge(consts, 7)
            v.tensor_copy(identb[:, :], ident[:, :]).then_inc(setup_v, 1)
            v.tensor_copy(relk[0:D, :], relk0[0:D, :]).then_inc(setup_v, 1)
            v.tensor_scalar(relk[D:P, :], relk0[D:P, :], 1.0, None, ALU.add).then_inc(setup_v, 1)
            v.wait_ge(resT, 1)
            v.wait_ge(setup_v, 8)
            for h in range(2):
                q = slice(h * D, (h + 1) * D)
                v.tensor_copy(bd_res[q, q], att_ps[q, 0:D]).then_inc(setup_v, 1)
                v.tensor_copy(bd_both[q, q], att_ps[q, D:2 * D]).then_inc(setup_v, 1)
            v.tensor_scalar(st_mix[:, :], att_ps[:, D:2 * D], SLOPE, None, ALU.mult).then_inc(setup_v, 1)
            v.wait_ge(setup_v, 15)
            v.scalar_tensor_tensor(bd_mix[:, :], bd_res[:, :], SLOPE, ident[:, :], ALU.mult, ALU.add).then_inc(setup_v, 1)
            v.wait_ge(dst_masked, 1)
            v.tensor_tensor(same[:, :], dst_f[:, 0:T], dst_f[:, 1:T + 1], ALU.is_equal).then_inc(setup_v, 1)
            v.tensor_scalar(inf_f[:, :], dst_f[:, 0:T], dst_f[:, 0:1], None, ALU.is_equal).then_inc(setup_v, 1)
            v.wait_ge(setup_v, 18)
            v.memset(start[:, 0:1], -BIG).then_inc(setup_v, 1)
            v.tensor_scalar(start[:, 1:T], same[:, 0:T - 1], -1.0, BIG, ALU.add, ALU.mult).then_inc(setup_v, 1)
            v.scalar_tensor_tensor(row_i[:, :], same[:, :], float(FAR), dst_f[:, 0:T], ALU.mult, ALU.add).then_inc(setup_v, 1)
            v.wait_ge(setup_v, SETUP_V)

            def mask(m, k):
                if k == 0:
                    v.wait_ge(xT_out, 2 * m.n + 2)
                    v.wait_ge(typ_out, m.n + 1)
                wait(v, pair_done, m.n * NK + k + 1 - XM)
                b = (m.slot * NK + k) % XM
                v.scalar_tensor_tensor(xm[:, b, :, :], typ[:, m.slot % 2, :].unsqueeze(1).to_broadcast([P, 2, W]),
                                       relk[:, k:k + 1], xT[:, m.slot % 2, :, :], ALU.is_equal, ALU.mult).then_inc(masked, 1)

            def guess(d, n):
                bits = newt[:, 0, :].bitcast(I32)
                wait(v, newt_step, d.n * 11 + n)
                if n == 0:
                    v.wait_ge(var_done, d.n + 1)
                    v.tensor_scalar(bits, var[:, d.slot, :].bitcast(I32), 1, None, ALU.logical_shift_right).then_inc(newt_step, 1)
                else:
                    v.tensor_scalar(rstd[:, d.slot, :].bitcast(I32), bits, -1.0, float(MAGIC), ALU.mult, ALU.add).then_inc(newt_step, 1)

            def sum_one(s, j):
                v.wait_ge(wx_done, s.n + 1)
                wait(v, sum_step, s.n * TG + j)
                c = s.n * TG + j
                v.scalar_tensor_tensor(es_all[:, bass.ds(c + 1, 1), :].rearrange("p a f -> p (a f)"),
                                       es_all[:, bass.ds(c, 1), :].rearrange("p a f -> p (a f)"),
                                       wd[:, s.slot % 2, 1, j:j + 1], wx[:, s.slot % 2, j, :],
                                       ALU.mult, ALU.add).then_inc(sum_step, 1)

            def refine(d, n):
                y, v_, a, b = rstd[:, d.slot, :], var[:, d.slot, :], newt[:, 0, :], newt[:, 1, :]
                v.wait_ge(newt_step, d.n * 11 + 2 + n)
                if n % 3 == 0:
                    v.tensor_tensor(a, y, y, ALU.mult).then_inc(newt_step, 1)
                elif n % 3 == 1:
                    v.scalar_tensor_tensor(b, a, -0.5, v_, ALU.mult, ALU.mult).then_inc(newt_step, 1)
                else:
                    v.scalar_tensor_tensor(y, b, 1.5, y, ALU.add, ALU.mult).then_inc(newt_step, 1)

            def score_max(a):
                v.wait_ge(att_done, a.n + 1)
                wait(v, max_done, a.n)
                v.tensor_tensor_scan(m_all[:, bass.ds(a.n * TG + 1, TG)], start[:, bass.ds(a.n * TG, TG)],
                                     att_ps[:, (a.slot % 2) * TG:(a.slot % 2) * TG + TG],
                                     m_all[:, bass.ds(a.n * TG, 1)], ALU.add, ALU.max).then_inc(max_done, 1)

            msk, aa = mats[:, 0, :], mats[:, 1, :]
            t2, mm, da, db, ea, eb = (tab[:, k * T:(k + 1) * T] for k in (2, 7, 3, 4, 5, 6))
            own, den = tab[:, 8 * T:9 * T], tab[:, 9 * T:10 * T]

            def exchange_max():
                v.wait_ge(ex_pe, 1)
                v.scalar_tensor_tensor(msk, typ_ps[:, P:2 * P], dst_f[:, 0:1], before[:, :], ALU.is_equal, ALU.mult).then_inc(ex_v, 1)
                v.wait_ge(ex_v, 1)
                v.tensor_tensor(aa, typ_ps[:, 0:P], msk, ALU.mult).then_inc(ex_v, 1)
                v.tensor_scalar(mats[:, 2, :], msk, -1.0, NONE, ALU.add, ALU.mult).then_inc(ex_w, 1)
                v.wait_ge(ex_v, 2)
                v.wait_ge(ex_w, 1)
                v.tensor_tensor(aa, aa, mats[:, 2, :], ALU.add).then_inc(ex_v, 1)
                v.wait_ge(ex_v, 3)
                v.tensor_reduce(prev[:, 0:1], aa, AX.X, ALU.max).then_inc(ex_v, 1)
                v.wait_ge(ex_v, 4)
                v.tensor_scalar(prev[:, 1:2], prev[:, 0:1], -1.0, None, ALU.mult).then_inc(ex_v, 1)
                v.wait_ge(z_done, NG)
                v.tensor_scalar(t2, inf_f[:, :], -1.0, NONE, ALU.add, ALU.mult).then_inc(ex_v, 1)
                v.wait_ge(ex_v, 6)
                v.scalar_tensor_tensor(own, inf_f[:, :], prev[:, 0:1], t2, ALU.mult, ALU.add).then_inc(ex_v, 1)
                v.wait_ge(ex_v, 7)
                v.tensor_tensor(mm, m_all[:, 1:T + 1], own, ALU.max).then_inc(ex_v, 1)
                v.wait_ge(ex_v, 8)
                v.tensor_tensor(da, m_all[:, 1:T + 1], mm, ALU.subtract).then_inc(ex_v, 1)
                v.tensor_tensor(db, own, mm, ALU.subtract).then_inc(ex_v, 1)

            def exchange_weights():
                v.wait_ge(ex_act, 1)
                v.tensor_tensor(mats[:, 3, :], mats[:, 2, :], msk, ALU.mult).then_inc(ex_v, 1)
                v.wait_ge(ex_pe, 2)
                v.tensor_copy(mats[:, 4, :], typ_ps[:, 2 * P:3 * P]).then_inc(ex_v, 1)

            def step(g):
                m, a, s, d, dv, dn = g.back(1), g.back(2), g.back(3), g.back(1), g.back(2), g.back(3)
                main, late, last = live(g, 1), live(g, 2), live(g, 3)
                if main:
                    mask(m, 0)
                if last:
                    guess(dn, 0)
                    sum_one(s, 0)
                    guess(dn, 1)
                if late:
                    v.wait_ge(tanh_done, a.n + 1)
                    wait(v, att_done, a.n - 1)
                    v.tensor_tensor(prod[:, a.slot % 2, :], th_ps[0:D, :], g_r[:, a.slot % 2, :],
                                    ALU.mult).then_inc(prod_done, 1)
                if last:
                    refine(dn, 0)
                if main:
                    mask(m, 1)
                if last:
                    refine(dn, 1)
                    sum_one(s, 1)
                    refine(dn, 2)
                if main:
                    mask(m, 2)
                if last:
                    refine(dn, 3)
                if last:
                    sum_one(s, 2)
                    refine(dn, 4)
                if main:
                    mask(m, 3)
                if late:
                    score_max(a)
                if last:
                    refine(dn, 5)
                if last:
                    sum_one(s, 3)
                if late:
                    b = a.slot % 2
                    col = bass.ds(a.n * TG + 1, TG)
                    v.wait_ge(max_done, a.n + 1)
                    wait(v, exp_done, a.n - 1)
                    v.tensor_tensor(delta[:, b, 1, :], m_all[:, bass.ds(a.n * TG, TG)], m_all[:, col],
                                    ALU.subtract).then_inc(sub_done, 1)
                    v.tensor_tensor(delta[:, b, 0, :], att_ps[:, (a.slot % 2) * TG:(a.slot % 2) * TG + TG],
                                    m_all[:, col], ALU.subtract)
                if last:
                    refine(dn, 6)
                if late:
                    v.wait_ge(sub_done, a.n + 1)
                    v.tensor_tensor(delta[:, b, 1, :], delta[:, b, 1, :], start[:, bass.ds(a.n * TG, TG)],
                                    ALU.add).then_inc(delta_done, 1)
                if known(g.turn) and g.n == NG + 1:
                    exchange_max()
                if main:
                    mask(m, 4)
                if last:
                    refine(dn, 7)
                if main:
                    wait(v, norm_done, d.n - RING + 1)
                    v.wait_ge(relu_done, d.n + 1)
                    v.tensor_tensor(z[:, d.slot, :], relu[:, d.slot % 2, :], y_ps[:, 1, :], ALU.add).then_inc(z_done, 1)
                if last:
                    refine(dn, 8)
                if late:
                    v.wait_ge(ssq_done, dv.n + 1)
                    v.tensor_scalar(var[:, dv.slot, :], ssq[:, dv.slot, :], 1.0 / D, EPS, ALU.mult, ALU.add).then_inc(var_done, 1)
                if main:
                    v.wait_ge(z_done, d.n + 1)
                    v.tensor_reduce(zsum[:, d.slot, :], z[:, d.slot, :].rearrange("p (j f) -> p j f", f=D), AX.X,
                                    ALU.add).then_inc(zsum_done, 1)
                if last:
                    v.wait_ge(newt_step, dn.n * 11 + 11)
                    v.tensor_tensor(nbias[:, dn.slot, :], nmean[:, dn.slot, :], rstd[:, dn.slot, :], ALU.mult).then_inc(bias_done, 1)
                    b = s.slot % 2
                    wait(v, den_done, s.n)
                    v.tensor_tensor_scan(s_all[:, bass.ds(s.n * TG + 1, TG)], wd[:, b, 1, :], wd[:, b, 0, :],
                                         s_all[:, bass.ds(s.n * TG, 1)], ALU.mult, ALU.add).then_inc(den_done, 1)
                if main:
                    v.wait_ge(zsum_done, d.n + 1)
                    v.tensor_scalar(nmean[:, d.slot, :], zsum[:, d.slot, :], -1.0 / D, None, ALU.mult).then_inc(mean_done, 1)
                if known(g.turn) and g.n == NG + 1:
                    exchange_weights()
            run_groups(v, step, NG, 3)

            v.wait_ge(ex_pe, 3)
            v.tensor_copy(carry[:, :], att_ps[:, P:P + D + 1]).then_inc(ex_v, 1)
            v.wait_ge(ex_act, 2)
            v.wait_ge(den_done, NG)
            v.tensor_tensor(own, ea, s_all[:, 1:T + 1], ALU.mult).then_inc(ex_v, 1)
            v.wait_ge(ex_v, 14)
            v.scalar_tensor_tensor(den, eb, carry[:, D:D + 1], own, ALU.mult, ALU.add).then_inc(ex_v, 1)
            v.wait_ge(ex_v, 15)
            v.reciprocal(mm, den).then_inc(ex_v, 1)
            v.wait_ge(ex_v, 16)
            v.tensor_tensor(fa, ea, mm, ALU.mult).then_inc(ex_v, 1)
            v.tensor_tensor(fb, eb, mm, ALU.mult).then_inc(ex_v, 1)
            v.wait_ge(ex_v, 18)

            for q in range(RING):
                v.wait_ge(xd_saved[q], -(-(NG - q) // RING) * DMA)

            def final(g):
                new, mid, var_, end = live(g), live(g, 2), live(g, 3), live(g, 4)
                b, dz, dv, de = g.slot % 2, g.back(2), g.back(3), g.back(4)
                c = dz.slot % 2
                cols = bass.ds(g.n * TG, TG)
                own_, car, h = (xT[:, b, k // 2, (k % 2) * 256:(k % 2) * 256 + 256].rearrange("p (j f) -> p j f", f=D)
                                for k in range(3))
                uw = xm[:, b, 0, :].rearrange("p (j k f) -> p j k f", k=2, f=D)
                r2 = relu[:, c, :].rearrange("p (j k f) -> p j k f", k=2, f=D)
                za, zb = (prod_ex[:, c, k, :] for k in range(2))
                if new:
                    wait(v, h_step, (g.n - 1) * 3)
                    v.tensor_tensor(own_, es_all[:, bass.ds(g.n * TG + 1, TG), :],
                                    fa[:, cols].unsqueeze(2).to_broadcast([P, TG, D]), ALU.mult).then_inc(h_step, 1)
                    v.tensor_tensor(car, carry[:, 0:D].unsqueeze(1).to_broadcast([P, TG, D]),
                                    fb[:, cols].unsqueeze(2).to_broadcast([P, TG, D]), ALU.mult).then_inc(h_step, 1)
                if end:
                    wait(v, scattered[de.slot], de.turn * TG * DMA)
                    v.tensor_copy(row_r[:, de.slot, :], row_i[:, bass.ds(de.n * TG, TG)]).then_inc(row_done, 1)
                    v.wait_ge(sqrt3_done, de.n + 1)
                    v.reciprocal(var[:, de.slot, 0:TG], rstd[:, de.slot, 0:TG]).then_inc(rec3_done, 1)
                if new:
                    v.wait_ge(h_step, g.n * 3 + 2)
                    v.tensor_tensor(h, own_, car, ALU.add).then_inc(h_step, 1)
                if end:
                    v.wait_ge(rec3_done, de.n + 1)
                    v.tensor_tensor(nbias[:, de.slot, 0:TG], nmean[:, de.slot, 0:TG], var[:, de.slot, 0:TG],
                                    ALU.mult).then_inc(bias3_done, 1)
                if mid:
                    v.wait_ge(relu3_done, dz.n + 1)
                    wait(v, z3_done, dz.n - 1)
                    v.tensor_tensor(za.rearrange("p (j f) -> p j f", f=D), r2[:, :, 0, :], r2[:, :, 1, :], ALU.add).then_inc(za_done, 1)
                    v.tensor_tensor(zb.rearrange("p (j f) -> p j f", f=D),
                                    y_ps[:, c, 0:TG * D].rearrange("p (j f) -> p j f", f=D),
                                    xd_all[:, bass.ds(dz.n * TG, TG), :], ALU.add).then_inc(za_done, 1)
                if new:
                    v.wait_ge(h_step, g.n * 3 + 3)
                    wait(v, uwT_done, g.n - 1)
                    xd = xd_all[:, cols, :]
                    v.tensor_tensor(uw[:, :, 0, :], h, xd, ALU.add)
                    v.tensor_tensor(uw[:, :, 1, :], h, xd, ALU.mult).then_inc(uw_done, 1)
                if var_:
                    v.wait_ge(sq3_done, dv.n + 1)
                    v.tensor_scalar(var[:, dv.slot, 0:TG], ssq[:, dv.slot, 0:TG], 1.0 / D, EPS, ALU.mult, ALU.add).then_inc(var3_done, 1)
                if mid:
                    v.wait_ge(za_done, 2 * dz.n + 2)
                    wait(v, norm3_done, dz.n - RING + 1)
                    v.tensor_tensor(z[:, dz.slot, 0:TG * D], za, zb, ALU.add).then_inc(z3_done, 1)
                if mid:
                    v.wait_ge(z3_done, dz.n + 1)
                    v.tensor_reduce(zsum[:, dz.slot, 0:TG], z[:, dz.slot, 0:TG * D].rearrange("p (j f) -> p j f", f=D), AX.X,
                                    ALU.add).then_inc(zsum3_done, 1)
                    v.wait_ge(zsum3_done, dz.n + 1)
                    v.tensor_scalar(nmean[:, dz.slot, 0:TG], zsum[:, dz.slot, 0:TG], -1.0 / D, None, ALU.mult).then_inc(mean3_done, 1)
            run_groups(v, final, NG, 4)


def kernel(**inputs):
    import numpy as np
    import concourse.bacc as bacc
    from concourse.bass_utils import run_bass_kernel_spmd

    nc = bacc.Bacc("TRN2", target_bir_lowering=False, num_devices=1)
    arrays, args = {}, []
    for name in ["x", "src", "dst", "edge_attr_64", "edge_type_10", "L0_gnn_relation_weight", "L0_gnn_res_fc_w",
                 "L0_gnn_res_fc2_w"]:
        a = np.ascontiguousarray(inputs[name])
        arrays[f"in_{name}"] = a
        args.append(nc.dram_tensor(f"in_{name}", a.shape, mybir.dt.from_np(a.dtype), kind="ExternalInput").ap())
    args.append(nc.dram_tensor("out", inputs["x"].shape, F32, kind="ExternalOutput").ap())
    gnn_resnorm(nc, *args)
    return run_bass_kernel_spmd(nc, [arrays], core_ids=[0]).results[0]["out"]
```
